# Optimizing a Trainium2 kernel written in Bass

```python
import numpy as np
import jax
import jax.numpy as jnp

def _softmax(x, axis=-1):
    return jax.nn.softmax(x, axis=axis)

def _gelu(x):
    return jax.nn.gelu(x, approximate=True)

def _silu(x):
    return jax.nn.silu(x)

def _sigmoid(x):
    return jax.nn.sigmoid(x)

def _layernorm(x, axis=-1, eps=1e-05):
    m = jnp.mean(x, axis=axis, keepdims=True)
    v = jnp.var(x, axis=axis, keepdims=True)
    return (x - m) / jnp.sqrt(v + eps)

def _scatter_add(tgt, idx, src, axis=0):
    return tgt.at[idx].add(src)

def _segment_sum(src, seg, n):
    return jax.ops.segment_sum(src, seg, n)
kernel_name = 'mk_vit_tower_cls_d1_tok_img256_r4_1a599e'

def setup_inputs(seed: int=0):
    np.random.seed(seed)
    _w = jnp.asarray

    def _rec_inputs():
        import jax
        import jax.numpy as jnp
        _rk = jax.random.key(seed)
        x = -0.000209053 + 0.999977 * jax.random.normal(jax.random.fold_in(_rk, 1), (4, 64, 56, 56), jnp.float32)
        cls_tok = 0.02 * jax.random.normal(jax.random.fold_in(_rk, 5), (1, 1, 64), jnp.float32)
        return (x, cls_tok)
    x, cls_tok = _rec_inputs()

    def _L0_tok_setup():
        import jax, jax.numpy as jnp
        import numpy as np
        B, EMB, HT, WD = (32, 64, 56, 56)
        NH, WS, SHIFTED = (8, 4, True)

        def _rel_indices(ws):
            coords = np.array([[i, j] for i in range(ws) for j in range(ws)])
            rel = coords[None, :, :] - coords[:, None, :] + ws - 1
            return jnp.asarray(rel)

        def _shift_masks(ws):
            m = np.zeros((ws * ws, ws * ws), np.float32)
            s = ws * (ws // 2)
            m[-s:, :-s] = -np.inf
            m[:-s, -s:] = -np.inf
            col = m.reshape(ws, ws, ws, ws).transpose(1, 0, 3, 2).reshape(ws * ws, ws * ws)
            return (jnp.asarray(m), jnp.asarray(col))
        key = jax.random.key(seed)
        ks = jax.random.split(key, 6)
        x = jax.random.normal(ks[0], (B, EMB, HT, WD), jnp.float32)
        s = 1.0 / np.sqrt(EMB)
        w1 = jax.random.uniform(ks[1], (3 * EMB, EMB), jnp.float32, -s, s)
        b1 = jax.random.uniform(ks[2], (3 * EMB,), jnp.float32, -s, s)
        w2 = jax.random.uniform(ks[3], (EMB, EMB), jnp.float32, -s, s)
        b2 = jax.random.uniform(ks[4], (EMB,), jnp.float32, -s, s)
        pos_emb = jax.random.normal(ks[5], (2 * WS - 1, 2 * WS - 1), jnp.float32)
        return {'x': x, 'w1': w1, 'b1': b1, 'w2': w2, 'b2': b2, 'pos_emb': pos_emb}
    _L0_tok_all = _L0_tok_setup()
    _L0_tok_in = {k: v for k, v in _L0_tok_all.items() if k in ('w1', 'b1', 'w2', 'b2', 'pos_emb')}
    del _L0_tok_all

    def _L0_attn_setup():
        import jax, jax.numpy as jnp
        import numpy as np
        C = 64
        key = jax.random.key(seed)
        ks = jax.random.split(key, 9)
        B, N = (4, 1024)
        s = 1.0 / np.sqrt(C)
        x = jax.random.normal(ks[0], (B, N, C), dtype=jnp.float32)
        g_w = jax.random.uniform(ks[1], (C, C), jnp.float32, -s, s)
        g_b = jax.random.uniform(ks[2], (C,), jnp.float32, -s, s)
        theta_w = jax.random.uniform(ks[3], (C, C), jnp.float32, -s, s)
        theta_b = jax.random.uniform(ks[4], (C,), jnp.float32, -s, s)
        phi_w = jax.random.uniform(ks[5], (C, C), jnp.float32, -s, s)
        phi_b = jax.random.uniform(ks[6], (C,), jnp.float32, -s, s)
        W_w = jax.random.uniform(ks[7], (C, C), jnp.float32, -s, s)
        W_b = jax.random.uniform(ks[8], (C,), jnp.float32, -s, s)
        return {'x': x, 'g_w': g_w, 'g_b': g_b, 'theta_w': theta_w, 'theta_b': theta_b, 'phi_w': phi_w, 'phi_b': phi_b, 'W_w': W_w, 'W_b': W_b}
    _L0_attn_all = _L0_attn_setup()
    _L0_attn_in = {k: v for k, v in _L0_attn_all.items() if k in ('g_w', 'g_b', 'theta_w', 'theta_b', 'phi_w', 'phi_b', 'W_w', 'W_b')}
    del _L0_attn_all

    def _L0_ffn_setup():
        import jax, jax.numpy as jnp
        import numpy as np
        B, S, D, H, E, K = (8, 2048, 64, 256, 8, 2)
        key = jax.random.key(seed)
        ks = jax.random.split(key, 7)
        s_in = 1.0 / np.sqrt(D)
        s_hid = 1.0 / np.sqrt(H)
        return {'x': jax.random.normal(ks[0], (B, S, D), dtype=jnp.float32), 'Wg': jax.random.uniform(ks[1], (E, D), jnp.float32, -s_in, s_in), 'bg': jax.random.uniform(ks[2], (E,), jnp.float32, -s_in, s_in), 'W1': jax.random.uniform(ks[3], (E, H, D), jnp.float32, -s_in, s_in), 'b1': jax.random.uniform(ks[4], (E, H), jnp.float32, -s_in, s_in), 'W2': jax.random.uniform(ks[5], (E, D, H), jnp.float32, -s_hid, s_hid), 'b2': jax.random.uniform(ks[6], (E, D), jnp.float32, -s_hid, s_hid)}
    _L0_ffn_all = _L0_ffn_setup()
    _L0_ffn_in = {k: v for k, v in _L0_ffn_all.items() if k in ('Wg', 'bg', 'W1', 'b1', 'W2', 'b2')}
    del _L0_ffn_all
    return {'x': x, 'cls_tok': cls_tok, 'L0_tok_w1': _L0_tok_in['w1'], 'L0_tok_b1': _L0_tok_in['b1'], 'L0_tok_w2': _L0_tok_in['w2'], 'L0_tok_b2': _L0_tok_in['b2'], 'L0_tok_pos_emb': _L0_tok_in['pos_emb'], 'L0_attn_g_w': _L0_attn_in['g_w'], 'L0_attn_g_b': _L0_attn_in['g_b'], 'L0_attn_theta_w': _L0_attn_in['theta_w'], 'L0_attn_theta_b': _L0_attn_in['theta_b'], 'L0_attn_phi_w': _L0_attn_in['phi_w'], 'L0_attn_phi_b': _L0_attn_in['phi_b'], 'L0_attn_W_w': _L0_attn_in['W_w'], 'L0_attn_W_b': _L0_attn_in['W_b'], 'L0_ffn_Wg': _L0_ffn_in['Wg'], 'L0_ffn_bg': _L0_ffn_in['bg'], 'L0_ffn_W1': _L0_ffn_in['W1'], 'L0_ffn_b1': _L0_ffn_in['b1'], 'L0_ffn_W2': _L0_ffn_in['W2'], 'L0_ffn_b2': _L0_ffn_in['b2']}

def reference(x, cls_tok, L0_tok_w1, L0_tok_b1, L0_tok_w2, L0_tok_b2, L0_tok_pos_emb, L0_attn_g_w, L0_attn_g_b, L0_attn_theta_w, L0_attn_theta_b, L0_attn_phi_w, L0_attn_phi_b, L0_attn_W_w, L0_attn_W_b, L0_ffn_Wg, L0_ffn_bg, L0_ffn_W1, L0_ffn_b1, L0_ffn_W2, L0_ffn_b2):
    import jax
    import jax.numpy as jnp

    def _L0_tok_ref(x, w1, b1, w2, b2, pos_emb):
        import jax, jax.numpy as jnp
        import numpy as np
        B, EMB, HT, WD = (32, 64, 56, 56)
        NH, WS, SHIFTED = (8, 4, True)

        def _rel_indices(ws):
            coords = np.array([[i, j] for i in range(ws) for j in range(ws)])
            rel = coords[None, :, :] - coords[:, None, :] + ws - 1
            return jnp.asarray(rel)

        def _shift_masks(ws):
            m = np.zeros((ws * ws, ws * ws), np.float32)
            s = ws * (ws // 2)
            m[-s:, :-s] = -np.inf
            m[:-s, -s:] = -np.inf
            col = m.reshape(ws, ws, ws, ws).transpose(1, 0, 3, 2).reshape(ws * ws, ws * ws)
            return (jnp.asarray(m), jnp.asarray(col))
        b, c, ht, wd = x.shape
        ws, nh = (WS, NH)
        e = c // nh
        xt = x.reshape(b, c, ht * wd).transpose(0, 2, 1)
        qkv = xt @ w1.T + b1
        qkv = qkv.reshape(b, ht, wd, c, 3)
        if SHIFTED:
            qkv = jnp.roll(qkv, (-ws // 2, -ws // 2), axis=(1, 2))
        Wh, Ww = (ht // ws, wd // ws)
        qkv = qkv.reshape(b, Wh, ws, Ww, ws, e, nh, 3)
        qkv = qkv.transpose(0, 6, 1, 3, 2, 4, 5, 7).reshape(b, nh, Wh, Ww, ws * ws, e, 3)
        Q, K, V = (qkv[..., 0], qkv[..., 1], qkv[..., 2])
        scale = jnp.sqrt(jnp.float32(c / nh))
        wei = jnp.einsum('bhijpe,bhijqe->bhijpq', Q, K) / scale
        rel = _rel_indices(ws)
        wei = wei + pos_emb[rel[..., 0], rel[..., 1]]
        if SHIFTED:
            row_mask, col_mask = _shift_masks(ws)
            wei = wei.at[:, :, -1, :].add(row_mask)
            wei = wei.at[:, :, :, -1].add(col_mask)
        attn = jax.nn.softmax(wei, axis=-1)
        out = jnp.einsum('bhijpq,bhijqe->bhijpe', attn, V)
        out = out.reshape(b, nh, Wh, Ww, ws, ws, e)
        out = out.transpose(0, 2, 4, 3, 5, 1, 6).reshape(b, ht, wd, nh * e)
        out = out.reshape(b, ht * wd, c)
        return out @ w2.T + b2

    def _L0_attn_ref(x, g_w, g_b, theta_w, theta_b, phi_w, phi_b, W_w, W_b):
        import jax, jax.numpy as jnp
        import numpy as np
        C = 64
        g_x = jnp.einsum('bnc,dc->bnd', x, g_w) + g_b
        theta_x = jnp.einsum('bnc,dc->bnd', x, theta_w) + theta_b
        phi_x = jnp.einsum('bnc,dc->bnd', x, phi_w) + phi_b
        N = x.shape[1]
        f = jnp.einsum('bic,bjc->bij', phi_x, theta_x) / N
        y = jnp.einsum('bij,bjc->bic', f, g_x)
        W_y = jnp.einsum('bnc,dc->bnd', y, W_w) + W_b
        return W_y + x

    def _L0_ffn_ref(x, Wg, bg, W1, b1, W2, b2):
        import jax, jax.numpy as jnp
        import numpy as np
        B, S, D, H, E, K = (8, 2048, 64, 256, 8, 2)
        gate_scores = jnp.einsum('bsd,ed->bse', x, Wg) + bg
        topk_scores, topk_idx = jax.lax.top_k(gate_scores, K)
        topk_probs = jax.nn.softmax(topk_scores, axis=-1)
        combine = jnp.sum(topk_probs[..., None] * jax.nn.one_hot(topk_idx, E, dtype=x.dtype), axis=-2)
        out = jnp.zeros_like(x)
        for e in range(E):
            h = jax.nn.relu(jnp.einsum('bsd,hd->bsh', x, W1[e]) + b1[e])
            y = jnp.einsum('bsh,dh->bsd', h, W2[e]) + b2[e]
            out = out + combine[..., e:e + 1] * y
        return out
    h = _L0_tok_ref(x, L0_tok_w1, L0_tok_b1, L0_tok_w2, L0_tok_b2, L0_tok_pos_emb)
    h = jnp.concatenate([jnp.broadcast_to(cls_tok, (h.shape[0], 1, h.shape[2])), h], axis=1)
    h = h + _L0_attn_ref(_layernorm(h, axis=-1), L0_attn_g_w, L0_attn_g_b, L0_attn_theta_w, L0_attn_theta_b, L0_attn_phi_w, L0_attn_phi_b, L0_attn_W_w, L0_attn_W_b)
    h = h + _L0_ffn_ref(_layernorm(h, axis=-1), L0_ffn_Wg, L0_ffn_bg, L0_ffn_W1, L0_ffn_b1, L0_ffn_W2, L0_ffn_b2)
    return h

_drawn_inputs = setup_inputs


def setup_inputs(seed=0):
    import zlib

    import numpy as np

    out = dict(_drawn_inputs(seed))
    spreads = {}
    factors = {'cls_tok': 2.684, 'L0_ffn_b1': 3.474, 'L0_ffn_b2': 2.771}
    for name, (base, spread) in spreads.items():
        noise = np.random.default_rng([zlib.crc32(name.encode()), seed]).standard_normal(out[name].shape)
        drawn = base * np.exp(spread * noise) if base else spread * noise
        out[name] = jnp.asarray(drawn.astype(out[name].dtype))
    for name, factor in factors.items():
        out[name] = (out[name] * factor).astype(out[name].dtype)
    return out
```

```python
from contextlib import ExitStack

import numpy as np

import concourse.bass as bass
from concourse import mybir

P = 128
F32 = mybir.dt.float32
F16 = mybir.dt.float16
ALU = mybir.AluOpType
ACT = mybir.ActivationFunctionType
AX = mybir.AxisListType.X

B, C, HT, WD = 4, 64, 56, 56
WS, NH, HE = 4, 8, 8
WIN = WS * WS
WROW = WD // WS
TOK = HT * WD
SEQ = TOK + 1
NW = 2 * WROW
NP = NW // 2
AT = NW * WIN
AB = B * (HT // WS) // 2
ABB = AB // B
T = 512
NT = T // P
NB = TOK // T
TAIL = TOK - NB * T
TW = TAIL + 1
E, HID = 8, 256
NM = HID // P
G1 = B * NB
EPS = 1e-5
SCALE = 1.0 / float(np.sqrt(np.float32(C / NH)))
MASKED = -1e30


def swin_linattn_moe(nc, x, wq, wk, wv, bq, bk, bv, w2, b2, pos, wmask, pairmask, headmask, ident, ident2,
                     cls, gw, gb, thw, phw, phb, ww, wb, wg, bg, f1, fb1, f2, fb2, lower, out):
    ctx = ExitStack()
    with ctx:
        def sb(name, shape, dt=F32):
            return ctx.enter_context(nc.sbuf_tensor(name, shape, dt))

        def sem(name):
            return ctx.enter_context(nc.semaphore(name))

        wst = sb("weights_f32", [P, 3 * P + 3 * C])
        wq_f, wk_f = wst[:, 0:P], wst[:, P:2 * P]
        wv_f, w2_f = wst[:, 2 * P:2 * P + C], wst[:, 2 * P + C:3 * P]
        wpk_h = sb("weights_h", [P, 3 * P + E], F16)
        wpk_l = sb("weights_l", [P, 3 * P + E], F16)
        wq_h, wk_h, wv_h, w2_h = wpk_h[:, 0:P], wpk_h[:, P:2 * P], wpk_h[:, 2 * P:2 * P + C], wpk_h[:, 2 * P + C:3 * P]
        wq_l, wk_l, wv_l, w2_l = wpk_l[:, 0:P], wpk_l[:, P:2 * P], wpk_l[:, 2 * P:2 * P + C], wpk_l[:, 2 * P + C:3 * P]
        wg_h, wg_l = wpk_h[:, 3 * P:3 * P + E], wpk_l[:, 3 * P:3 * P + E]
        bias_q, bias_k, bias_v = sb("bias_q", [P, 1]), sb("bias_k", [P, 1]), sb("bias_v", [P, P])
        b2_bc = sb("b2_bc", [P, C])
        pos_sb = sb("pos_sb", [P, WIN])
        score_bias = sb("score_bias", [P, 3 * WROW, WIN])
        pair_m = sb("pair_m", [P, 2])
        head_m = sb("head_m", [P, NH])
        id_h = sb("id_h", [P, P], F16)
        id2 = sb("id2", [P, C])
        gw_sb, gb_sb = sb("gw_sb", [P, C]), sb("gb_sb", [1, C])
        th_sb, ph_sb, phb_sb = sb("th_sb", [C + 1, C]), sb("ph_sb", [C, P]), sb("phb_sb", [C, P])
        ww_sb, wb_bc = sb("ww_sb", [C, C]), sb("wb_bc", [P, C])
        bg_bc = sb("bg_bc", [P, E])
        low_m = sb("low_m", [P, E * E])
        half_neg, inv_c = sb("half_neg", [P, NT]), sb("inv_c", [P, NT])
        w1_h = sb("w1_h", [P, E * HID], F16)
        w1_l = sb("w1_l", [P, E * HID], F16)
        f2_h = sb("f2_h", [P, E * NM, C], F16)
        f2_l = sb("f2_l", [P, E * NM, C], F16)
        fb2_sb = sb("fb2_sb", [P, E * C], F16)
        one_rows = sb("one_rows", [P, P], F16)
        img = sb("img", [P, 2 * HT, WD])
        xs = [sb(f"xs{i}", [P, AT], F16) for i in range(2)]
        xrep = sb("xrep", [P, NP, 4, 2 * WIN], F16)
        k_h, k_l = sb("k_h", [P, AT], F16), sb("k_l", [P, AT], F16)
        q_s = sb("q_s", [P, AT], F16)
        spread_buf = sb("spread_buf", [P, 4, NW * P], F16)
        qx = [spread_buf[:, i, :].rearrange("p (w h q) -> p w h q", h=NH, q=WIN) for i in range(2)]
        sc = [sb(f"sc{i}", [P, AT]) for i in range(2)]
        smax, ssum, srec = sb("smax", [P, NW]), sb("ssum", [P, NW]), sb("srec", [P, NW])
        prt = sb("prt", [P, AT])
        pt_h, pt_l = sb("pt_h", [P, AT], F16), sb("pt_l", [P, AT], F16)
        px_h = [sb(f"px_h{i}", [P, NP, 2, 2, WIN], F16) for i in range(2)]
        px_l = [sb(f"px_l{i}", [P, NP, 2, 2, WIN], F16) for i in range(2)]
        vx = [spread_buf[:, 2 + i, :].rearrange("p (n a c) -> p n a c", a=2, c=P) for i in range(2)]
        o_h = sb("o_h", [P, B * TOK], F16)
        o_l = sb("o_l", [P, B * TOK], F16)
        res = sb("res", [P, B * NB * NT, C])
        res_t = sb("res_t", [P, B, C])
        x1t = spread_buf[:, :, :].rearrange("p i n -> p (i n)")[:, 0:B * NB * T].rearrange("p (r n) -> p r n", n=T)
        x1t_t = sb("x1t_t", [P, B * TW + P], F16)
        xt = [sb(f"xt{i}", [P, NT, P + 2], F16) for i in range(2)]
        ln_a, ln_q, ln_n = sb("ln_a", [P, NT, C]), sb("ln_q", [P, NT, C]), sb("ln_n", [P, NT, C])
        ln_s, ln_m, ln_v, ln_r = sb("ln_s", [P, NT]), sb("ln_m", [P, NT]), sb("ln_v", [P, NT]), sb("ln_r", [P, NT])
        gram = sb("gram", [P, P + 1])
        gcol = sb("gcol", [P, C + 1])
        grow = sb("grow", [1, C + 1])
        t1, ft, fw = sb("t1", [C + 1, C]), sb("ft", [C, C]), sb("fw", [C, C])
        mp_f = sb("mp_f", [P, C])
        mp_h, mp_l = sb("mp_h", [P, B, C], F16), sb("mp_l", [P, B, C], F16)
        cvec = sb("cvec", [P, B, C])
        h2 = [sb(f"h2{i}", [P, NT, C]) for i in range(2)]
        xa = [sb(f"xa{i}", [P, T], F16) for i in range(2)]
        xb = [sb(f"xb{i}", [P, T], F16) for i in range(2)]
        gs = sb("gs", [P, NT, E])
        gcmp, geq = sb("gcmp", [P, NT, E * E]), sb("geq", [P, NT, E * E])
        gcnt, gmx, gex = sb("gcnt", [P, NT * E]), sb("gmx", [P, NT]), sb("gex", [P, NT, E])
        gsum, grec = sb("gsum", [P, NT]), sb("grec", [P, NT])
        comb = [sb(f"comb{i}", [P, NT, E]) for i in range(2)]
        hh = [sb(f"hh{i}", [P, NM, T], F16) for i in range(2)]
        hl = [sb(f"hl{i}", [P, NM, T], F16) for i in range(2)]
        ye = [sb(f"ye{i}", [P, NT, C]) for i in range(2)]
        yc = sb("yc", [P, NT, C])
        acc = [sb(f"acc{i}", [P, NT, C]) for i in range(2)]
        flat = img[:, :, :].rearrange("p a b -> p (a b)")
        w1_f = flat[:, 0:E * HID]
        f2_f = flat[:, E * HID:E * HID + E * NM * C]
        fb1_f = flat[:, HT * WD:HT * WD + E * HID]
        fb2_f = flat[:, HT * WD + E * HID:HT * WD + E * HID + E * C]

        ps = ctx.enter_context(nc.psum_tensor("ps", [P, 8 * 512], F32))

        def bank(i, n=1):
            return ps[:, 512 * i:512 * (i + n)]

        ps_q, ps_k, ps_v = bank(0)[:, 0:AT], bank(1)[:, 0:AT], bank(2, 2)
        ps_s = [bank(4)[:, 0:AT], bank(5)[:, 0:AT]]
        ps_o = [bank(6)[:, 0:AT], bank(7)[:, 0:AT]]
        ps_h = [bank(0), bank(1)]
        ps_g = [bank(4 + b)[:, 0:P + 1] for b in range(B)]
        ps_ye = [bank(4), bank(5)]
        ps_t2 = bank(6).bitcast(F16)[:, 0:NT * P]
        ps_y, ps_gate = bank(7)[:, 0:NT * C], bank(7)[:, NT * C:NT * C + NT * E]
        ACT_HEADS = 4

        def ps_t1(u):
            return bank(2 + u).bitcast(F16)[:, 0:NT * P]

        def z_src(e, n):
            return bank(2 * (e % 2), 2).rearrange("p (m n) -> p m n", m=NM)[:, :, 0:n]

        def y_src(e, w, nt):
            return ps_ye[e % 2][0:w, 0:nt * C].rearrange("p (t c) -> p t c", c=C)

        def v_src(hp):
            return ps_v[32 * hp:32 * hp + 32, 0:NP * C].rearrange("p (n a h e) -> p n a h e", a=2, e=HE, h=NH // 2)[:, :, :, hp, :]

        def v_diag(u, hp, lo):
            base = vx[u][32 * hp:32 * hp + 32]
            return bass.AP(base.tensor, base.offset + lo * C + hp * HE,
                           [list(base.ap[0]), [2 * P, NP], [P + C // 2, 2], [1, HE]])

        def o_src(u, ip):
            return ps_o[u][:, ip * AT // 2:(ip + 1) * AT // 2].rearrange("p (j a b) -> p j a b", a=WS, b=WS)

        def o_dst(buf, g, ip):
            return buf[:, bass.ds(g * AT + ip * AT // 2, AT // 2)].rearrange("p (a j b) -> p j a b", a=WS, b=WS)

        names = ("consts img split img_free xs_ready xs_lo xrep_ready k_hi k_lo q_hi q_lo qx_dve qx_act "
                 "qk_done v_done s_done o_done v_hi v_lo sc_ready max_ready shift_ready exp_ready sum_ready rec_ready "
                 "norm_ready pt_ready pt_hi pt_lo px_ready o_hi o_lo sbias zeros "
                 "h_done h_ready lsum lmean lcent lsq lvar lveps lrstd lnorm lhi llo t_done t_copied g_done "
                 "mA mB dstep y_done y_ready cadd xT_ready xa_ready xb_ready gate_done gate_ready gstep comb_ready selected gsel mp_hi cls_in kept vb_done vb_ready gexp "
                 "z_done h_hi h_lo e_done ye_ready yc_ready acc_ready stored0 stored1 fw_load fw_stage fw_prep acc_init").split()
        S = {n: sem(n) for n in names}
        block = ctx.enter_context(nc.Block())

        class Step:
            def __init__(self, eng, name):
                self.eng, self.name, self.n = eng, name, 0

            def do(self, ins):
                self.n += 1
                ins.then_inc(S[self.name], 1)

            def done(self):
                self.eng.wait_ge(S[self.name], self.n)

        CONSTS = [(wq_f, wq), (wk_f, wk), (wv_f, wv), (w2_f, w2), (wst[:, 3 * P:3 * P + E], wg), (bias_q, bq), (bias_k, bk), (bias_v, bv),
                  (b2_bc, b2), (pos_sb, pos), (pair_m, pairmask), (head_m, headmask), (id_h, ident), (id2, ident2),
                  (score_bias[:, :, :].rearrange("p a b -> p (a b)"), wmask), (gw_sb, gw), (gb_sb, gb), (th_sb, thw),
                  (ph_sb, phw), (phb_sb, phb), (ww_sb, ww), (wb_bc, wb), (bg_bc, bg), (low_m, lower)]
        CONST_WAIT = 16 * len(CONSTS) + 16

        def full(t):
            return t[:, :] if hasattr(t, "shape") and len(t.shape) == 2 else t

        def load_image(eng, b):
            s = WS // 2
            if b:
                eng.wait_ge(S["img"], IMG * b)
            for half in range(2):
                d = img[C * half:C * half + C, HT * (b % 2):HT * (b % 2) + HT, :]
                for (dy, sy, ny) in ((0, s, HT - s), (HT - s, 0, s)):
                    for (dx, sx, nx) in ((0, s, WD - s), (WD - s, 0, s)):
                        eng.dma_start(d[:, dy:dy + ny, dx:dx + nx],
                                      x[b, :, sy:sy + ny, sx:sx + nx]).then_inc(S["img"], 16)

        IMG = 8 * 16

        def attn_steps(stages, mid):
            depth = max(l for _, l in stages)
            lead = depth + depth % 2 + 2
            total = AB + depth

            def step(s, u, check):
                for fn, lag in stages:
                    if check and not 0 <= s - lag < AB:
                        continue
                    fn(s - lag, (u - lag) % 2)
            for s in range(lead):
                step(s, s % 2, True)
            trips = (AB - lead) // 2
            with mid(0, trips) as i:
                for u in range(2):
                    step(i * 2 + (lead + u), u, False)
            for s in range(lead + 2 * trips, total):
                step(s, s % 2, True)

        def past(g, n):
            return not isinstance(g, int) or g >= n

        @block.sync
        def _(sp):
            load_image(sp, 0)
            for dst, src in CONSTS:
                sp.dma_start(full(dst), src).then_inc(S["consts"], 16)
            sp.dma_start(res_t[TAIL:TW, :, :], cls).then_inc(S["consts"], 16)
            load_image(sp, 1)
            for b in range(2, B):
                sp.wait_ge(S["xs_lo"], 2 * ABB * (b - 1))
                load_image(sp, b)
            sp.wait_ge(S["xs_lo"], 2 * AB)
            sp.dma_start(w1_f, f1).then_inc(S["fw_load"], 16)
            sp.dma_start(f2_f, f2).then_inc(S["fw_load"], 16)
            for r in (64, 96):
                sp.dma_start(fb1_f[r:r + 1, :], fb1).then_inc(S["fw_load"], 16)
            for r in (0, 32):
                sp.dma_start(fb2_f[r:r + 1, :], fb2).then_inc(S["fw_load"], 16)

            def store(b, r, u, n):
                sp.wait_ge(S["acc_ready"], n)
                base = b * SEQ + 1 + r * T
                sp.dma_start(out[bass.ds(base, T), :].rearrange("(t p) c -> p t c", p=P),
                             acc[u][:, :, :]).then_inc(S[f"stored{u}"], 16)
            for b in range(B):
                with sp.Fori(0, NB // 2) as i:
                    for u in range(2):
                        r = i * 2 + u
                        store(b, r, u, E * (r + b * NB + 1))
            sp.wait_ge(S["acc_ready"], E * (B * NB + 1))
            for b in range(B):
                sp.dma_start(out[b * SEQ + 1 + NB * T:(b + 1) * SEQ, :], acc[0][0:TAIL, b, :]).then_inc(S["stored0"], 16)
                sp.dma_start(out[b * SEQ:b * SEQ + 1, :], acc[0][TAIL:TW, b, :]).then_inc(S["stored0"], 16)
            sp.wait_ge(S["stored0"], 16 * (G1 // 2 + 2 * B))
            sp.wait_ge(S["stored1"], 16 * (G1 // 2))

        def ln_pool_centre(pool, src, m, w, nt):
            pool.wait_ge(S["lsum"], m)
            nc.gpsimd.tensor_tensor(ln_m[0:w, 0:nt], ln_s[0:w, 0:nt], inv_c[0:w, 0:nt], ALU.mult).then_inc(S["lmean"], 1)
            pool.wait_ge(S["lmean"], m)
            nc.gpsimd.tensor_tensor(ln_a[0:w, 0:nt, :], src, ln_m[0:w, 0:nt, None].broadcast_to([w, nt, C]),
                                    ALU.subtract).then_inc(S["lcent"], 1)

        def ln_pool_scale(pool, dst, m, w, nt, free=None):
            pool.wait_ge(S["lveps"], m)
            nc.gpsimd.tensor_tensor(ln_r[0:w, 0:nt], ln_v[0:w, 0:nt], half_neg[0:w, 0:nt], ALU.pow).then_inc(S["lrstd"], 1)
            pool.wait_ge(S["lrstd"], m)
            nc.gpsimd.tensor_tensor(ln_n[0:w, 0:nt, :], ln_a[0:w, 0:nt, :], ln_r[0:w, 0:nt, None].broadcast_to([w, nt, C]),
                                    ALU.mult).then_inc(S["lnorm"], 1)
            pool.wait_ge(S["lhi"], m)
            nc.gpsimd.tensor_tensor(dst[0:w, 0:nt, C:P], ln_n[0:w, 0:nt, :], dst[0:w, 0:nt, 0:C],
                                    ALU.subtract).then_inc(S["llo"], 1)

        def ln_dve_sum(dve, src, w, nt):
            nc.vector.reduce_sum(ln_s[0:w, 0:nt], src, AX).then_inc(S["lsum"], 1)

        def ln_dve_var(dve, m, w, nt):
            dve.wait_ge(S["lsq"], m)
            nc.vector.reduce_sum(ln_v[0:w, 0:nt], ln_q[0:w, 0:nt, :], AX).then_inc(S["lvar"], 1)
            dve.wait_ge(S["lvar"], m)
            nc.vector.tensor_scalar(ln_v[0:w, 0:nt], ln_v[0:w, 0:nt], 1.0 / C, EPS, ALU.mult,
                                    ALU.add).then_inc(S["lveps"], 1)

        def ln_act_square(act, m, w, nt):
            act.wait_ge(S["lcent"], m)
            nc.scalar.activation(ln_q[0:w, 0:nt, :], ln_a[0:w, 0:nt, :], ACT.Square).then_inc(S["lsq"], 1)

        def ln_act_hi(act, dst, m, w, nt):
            act.wait_ge(S["lnorm"], m)
            nc.scalar.activation(dst[0:w, 0:nt, 0:C], ln_n[0:w, 0:nt, :], ACT.Copy).then_inc(S["lhi"], 1)



        def blocks_of(engine, fn, lead_b=None):
            for u in range(2):
                fn(u, u, P, NT)
            with engine.Fori(1, G1 // 2) as i:
                for u in range(2):
                    fn(i * 2 + u, u, P, NT)
            fn(G1, 0, TW, B)

        MB = 7

        def expert_blocks(engine, prep, body):
            full, tail = (P, NT), (TW, B)

            def one(r, u, shape, ahead):
                for e in range(E + 1):
                    body(e, r, u, *shape)
                    if ahead:
                        for at, piece in prep:
                            if at == e:
                                piece(r + 1, 1 - u, *ahead)
            for _, piece in prep:
                piece(0, 0, *full)
            for u in range(2):
                one(u, u, full, full)
            with engine.Fori(1, G1 // 2 - 1) as i:
                for u in range(2):
                    one(i * 2 + u, u, full, full)
            one(G1 - 2, 0, full, full)
            one(G1 - 1, 1, full, tail)
            one(G1, 0, tail, None)

        class Chain:
            def __init__(self, eng, name, per):
                self.eng, self.name, self.per = eng, name, per

            def start(self, r):
                self.r, self.n = r, 0

            def do(self, ins):
                ins.then_inc(S[self.name], 1)
                self.n += 1
                assert self.n <= self.per
                self.eng.wait_ge(S[self.name], self.r * self.per + self.n)

        @block.gpsimd
        def _(pool):
            zeros = Step(pool, "zeros")
            fills = [(vx[0][:, :, :, :], 0.0), (vx[1][:, :, :, :], 0.0), (half_neg[:, :], -0.5), (inv_c[:, :], 1.0 / C),
                     (one_rows[:, :], 0.0), (fb2_sb[:, :], 0.0), (x1t_t[:, B * TW:B * TW + P], 0.0)]
            fills += [(t[:, :, P:P + 2], 1.0) for t in xt] + [(t[C:P, :], 0.0) for t in xb]
            fills += [(t[r:r + 1, :], 1.0) for t in xb for r in (64, 96)] + [(one_rows[r:r + 1, :], 1.0) for r in (0, 32)]
            for dst, value in fills:
                zeros.do(nc.gpsimd.memset(dst, value))
                zeros.done()

            def take_tokens(g, u):
                pool.wait_ge(S["img"], IMG * (g // ABB + 1))
                if past(g, 2):
                    pool.wait_ge(S["qk_done"], g - 1)
                    pool.wait_ge(S["xrep_ready"], g - 1)
                def rows(p0, ip):
                    return img[p0:P, bass.ds(g % (2 * ABB) * (2 * WS) + ip * WS, WS), :]\
                        .rearrange("c a (j b) -> c j a b", b=WS)

                def dst(p0, ip):
                    return xs[u][p0:P, ip * AT // 2:(ip + 1) * AT // 2]\
                        .rearrange("c (j a b) -> c j a b", a=WS, b=WS)
                for ip in range(2):
                    nc.gpsimd.tensor_copy(dst(0, ip), rows(0, ip)).then_inc(S["xs_ready"], 1)
                pool.wait_ge(S["xs_ready"], g * 2 + 2)
                for ip in range(2):
                    nc.gpsimd.tensor_tensor(dst(C, ip), rows(C, ip), dst(C, ip), ALU.subtract).then_inc(S["xs_lo"], 1)
                pool.wait_ge(S["xs_lo"], g * 2 + 2)

            def shift(g, u):
                pool.wait_ge(S["max_ready"], g + 1)
                s3 = sc[u][:, :].rearrange("p (w k) -> p w k", k=WIN)
                nc.gpsimd.tensor_tensor(s3, s3, smax[:, :, None].broadcast_to([P, NW, WIN]),
                                        ALU.subtract).then_inc(S["shift_ready"], 1)

            def normalise(g, u):
                pool.wait_ge(S["rec_ready"], g + 1)
                s3 = sc[u][:, :].rearrange("p (w k) -> p w k", k=WIN)
                nc.gpsimd.tensor_tensor(s3, s3, srec[:, :, None].broadcast_to([P, NW, WIN]),
                                        ALU.mult).then_inc(S["norm_ready"], 1)

            def low_part(g, u):
                pool.wait_ge(S["pt_hi"], g + 1)
                if past(g, 1):
                    pool.wait_ge(S["px_ready"], g)
                nc.gpsimd.tensor_tensor(pt_l[:, :], prt[:, :], pt_h[:, :], ALU.subtract).then_inc(S["pt_lo"], 1)

            attn_steps([(shift, 2), (take_tokens, 0), (normalise, 2), (low_part, 2)], pool.Fori)

            def ln1(r, u, w, nt):
                m = r + 1
                ln_pool_centre(pool, h2[u][0:w, 0:nt, :], m, w, nt)
                ln_pool_scale(pool, xt[u], m, w, nt)
            blocks_of(pool, ln1)

            pool.wait_ge(S["kept"], G1 + 1)

            def mix_const(b):
                pool.wait_ge(S["mB"], MB * (b + 1))
                nc.gpsimd.tensor_tensor(res_t[0:TW, b, :], res_t[0:TW, b, :], cvec[0:TW, b, :],
                                        ALU.add).then_inc(S["cadd"], 1)
                with pool.Fori(0, NB) as r:
                    rows = res[:, bass.ds(r * NT + b * NB * NT, NT), :]
                    nc.gpsimd.tensor_tensor(rows, rows, cvec[:, b:b + 1, :].broadcast_to([P, NT, C]),
                                            ALU.add).then_inc(S["cadd"], 1)

            def ln2(r, u, w, nt):
                m = r + G1 + 2
                src = h2[u][0:w, 0:nt, :]
                ln_pool_centre(pool, src, m, w, nt)
                ln_pool_scale(pool, xt[u], m, w, nt)

            def combine(r, u, w, nt, e):
                k = r * E + e
                pool.wait_ge(S["ye_ready"], k + 1)
                if e == 0:
                    pool.wait_ge(S["comb_ready"], r + 1)
                if past(k, 1):
                    pool.wait_ge(S["acc_ready"], k)
                nc.gpsimd.tensor_tensor(yc[0:w, 0:nt, :], ye[e % 2][0:w, 0:nt, :],
                                        comb[u][0:w, 0:nt, e:e + 1].broadcast_to([w, nt, C]), ALU.mult).then_inc(S["yc_ready"], 1)
                pool.wait_ge(S["yc_ready"], k + 1)
                if e == 0 and past(r, 2):
                    pool.wait_ge(S[f"stored{u}"], r // 2 * 16)
                first = h2[u][0:w, 0:nt, :] if e == 0 else acc[u][0:w, 0:nt, :]
                nc.gpsimd.tensor_tensor(acc[u][0:w, 0:nt, :], first, yc[0:w, 0:nt, :], ALU.add).then_inc(S["acc_ready"], 1)

            for b in range(B):
                mix_const(b)
            expert_blocks(pool, [(2, ln2)], lambda e, *blk: combine(*blk, e - 1) if e else None)

        @block.scalar
        def _(act):
            act.wait_ge(S["consts"], CONST_WAIT)
            act.wait_ge(S["zeros"], 2)
            act.wait_ge(S["split"], 1)

            def k_high(g, u):
                act.wait_ge(S["qk_done"], g + 1)
                if past(g, 1):
                    act.wait_ge(S["s_done"], g)
                nc.scalar.activation(k_h[:, :], ps_k, ACT.Identity, bias=bias_k[:, :]).then_inc(S["k_hi"], 1)
                if past(g, 1):
                    act.wait_ge(S["qx_dve"], g)
                nc.scalar.activation(q_s[:, :], ps_q, ACT.Identity, bias=bias_q[:, :]).then_inc(S["q_hi"], 1)

            def spread(g, u):
                act.wait_ge(S["q_lo"], g + 1)
                if past(g, 2):
                    act.wait_ge(S["s_done"], g - 1)
                q3 = q_s[:, :].rearrange("p (w q) -> p w q", q=WIN)
                for h in range(ACT_HEADS):
                    ins = nc.scalar.activation(qx[u][:, :, h, :], q3, ACT.Copy, scale=head_m[:, h:h + 1])
                ins.then_inc(S["qx_act"], 1)

            def v_high(g, u):
                act.wait_ge(S["v_done"], g + 1)
                if past(g, 2):
                    act.wait_ge(S["o_done"], g - 1)
                for hp in range(4):
                    nc.scalar.activation(v_diag(u, hp, 0), v_src(hp), ACT.Copy).then_inc(S["v_hi"], 1)

            def exp(g, u):
                act.wait_ge(S["shift_ready"], g + 1)
                nc.scalar.activation(sc[u][:, :], sc[u][:, :], ACT.Exp).then_inc(S["exp_ready"], 1)

            def p_high(g, u):
                act.wait_ge(S["pt_ready"], g + 1)
                if past(g, 1):
                    act.wait_ge(S["px_ready"], g)
                nc.scalar.activation(pt_h[:, :], prt[:, :], ACT.Copy).then_inc(S["pt_hi"], 1)

            def o_high(g, u):
                act.wait_ge(S["o_done"], g + 1)
                for ip in range(2):
                    nc.scalar.activation(o_dst(o_h, g, ip), o_src(u, ip), ACT.Copy).then_inc(S["o_hi"], 1)
            attn_steps([(exp, 2), (v_high, 2), (k_high, 1), (spread, 1), (p_high, 2), (o_high, 3)], act.Fori)

            def ln1(r, u, w, nt):
                m = r + 1
                act.wait_ge(S["h_ready"], m)
                if w == P:
                    ins = nc.scalar.activation(res[:, bass.ds(r * NT, NT), :], h2[u][:, :, :], ACT.Copy)
                else:
                    ins = nc.scalar.activation(res_t[0:TAIL, :, :], h2[u][0:TAIL, :, :], ACT.Copy)
                ins.then_inc(S["kept"], 1)
                if past(r, 1):
                    act.wait_ge(S["lvar"], r)
                ln_act_square(act, m, w, nt)
                if past(r, 2):
                    act.wait_ge(S["g_done"], r - 1)
                ln_act_hi(act, xt[u], m, w, nt)
                act.wait_ge(S["t_done"], r + 1)
                src = ps_t1(u)
                if w == P:
                    ins = nc.scalar.activation(x1t[:, bass.ds(r, 1), :].rearrange("p a b -> p (a b)"), src, ACT.Copy)
                else:
                    ins = nc.scalar.activation(x1t_t[:, 0:B * TW].rearrange("p (t n) -> p t n", n=TW),
                                               src.rearrange("p (t n) -> p t n", n=P)[:, :, 0:TW], ACT.Copy)
                ins.then_inc(S["t_copied"], 1)
            blocks_of(act, ln1)

            def square(r, u, w, nt):
                act.wait_ge(S["lvar"], r + G1 + 1)
                ln_act_square(act, r + (G1 + 2), w, nt)

            def high(r, u, w, nt):
                if past(r, 2):
                    act.wait_ge(S["t_done"], r + G1)
                ln_act_hi(act, xt[u], r + (G1 + 2), w, nt)

            def columns(r, u, w, nt):
                act.wait_ge(S["t_done"], r + (G1 + 2))
                if past(r, 2):
                    act.wait_ge(S["z_done"], (r - 1) * E)
                    act.wait_ge(S["gate_done"], r - 1)
                src = ps_t2.rearrange("p (t n) -> p t n", n=P)[:, 0:nt, 0:w]
                n = w * nt
                nc.scalar.activation(xa[u][:, 0:n].rearrange("p (t n) -> p t n", n=w), src, ACT.Copy).then_inc(S["xa_ready"], 1)
                nc.scalar.activation(xb[u][0:C, 0:n].rearrange("p (t n) -> p t n", n=w), src[0:C], ACT.Copy).then_inc(S["xb_ready"], 1)

            def gate_exp(r, u, w, nt):
                act.wait_ge(S["selected"], r + 1)
                nc.scalar.activation(gex[0:w, 0:nt, :], gex[0:w, 0:nt, :], ACT.Exp).then_inc(S["gexp"], 1)

            def expert(e, r, u, w, nt):
                n = w * nt
                if e < E:
                    k = r * E + e
                    act.wait_ge(S["z_done"], k + 1)
                    if past(r, 1) or e >= 2:
                        act.wait_ge(S["e_done"], k - 1)
                    nc.scalar.activation(hh[e % 2][:, :, 0:n], z_src(e, n), ACT.Relu).then_inc(S["h_hi"], 1)
                if e:
                    k = r * E + (e - 1)
                    act.wait_ge(S["e_done"], k + 1)
                    if past(r, 1) or e >= 3:
                        act.wait_ge(S["yc_ready"], k - 1)
                    nc.scalar.activation(ye[(e - 1) % 2][0:w, 0:nt, :], y_src(e - 1, w, nt), ACT.Copy).then_inc(S["ye_ready"], 1)
            expert_blocks(act, [(2, square), (4, high), (6, columns), (8, gate_exp)], expert)

        @block.vector
        def _(dve):
            dve.wait_ge(S["consts"], CONST_WAIT)
            steps = Step(dve, "sbias")
            nf = 3 * P + E
            steps.do(nc.vector.tensor_copy(wpk_h[:, 0:nf], wst[:, 0:nf]))
            steps.do(nc.vector.tensor_tensor(score_bias[:, :, :], score_bias[:, :, :],
                                             pos_sb[:, None, :].broadcast_to([P, 3 * WROW, WIN]), ALU.add))
            steps.do(nc.vector.memset(grow[:, C:C + 1], float(SEQ)))
            steps.done()
            nc.vector.tensor_tensor(wpk_l[:, 0:nf], wst[:, 0:nf], wpk_h[:, 0:nf], ALU.subtract).then_inc(S["split"], 1)
            dve.wait_ge(S["zeros"], 2)
            dve.wait_ge(S["vb_done"], 1)
            nc.vector.tensor_tensor(b2_bc[:, :], bank(7)[:, 0:C], b2_bc[:, :], ALU.add).then_inc(S["vb_ready"], 1)

            def scores(g, u):
                dve.wait_ge(S["s_done"], g + 1)
                last = g % ABB // (ABB - 1) * WROW
                nc.vector.scalar_tensor_tensor(
                    sc[u][:, :].rearrange("p (w k) -> p w k", k=WIN), ps_s[u].rearrange("p (w k) -> p w k", k=WIN),
                    SCALE, score_bias[:, bass.ds(last, NW), :], ALU.mult, ALU.add).then_inc(S["sc_ready"], 1)
                dve.wait_ge(S["sc_ready"], g + 1)
                nc.vector.reduce_max(smax[:, :], sc[u][:, :].rearrange("p (w k) -> p w k", k=WIN), AX)\
                    .then_inc(S["max_ready"], 1)

            def replicate(g, u):
                dve.wait_ge(S["xs_lo"], g * 2 + 2)
                if past(g, 1):
                    dve.wait_ge(S["v_done"], g)
                nc.vector.tensor_copy(xrep[:, :, :, :], xs[u][:, :].rearrange("p (a b) -> p a b", b=2 * WIN)
                                      [:, :, None, :].broadcast_to([P, NP, 4, 2 * WIN])).then_inc(S["xrep_ready"], 1)

            def v_low(g, u):
                for hp in range(4):
                    dve.wait_ge(S["v_hi"], g * 4 + (hp + 1))
                    ins = nc.vector.tensor_tensor(v_diag(u, hp, 1), v_src(hp), v_diag(u, hp, 0), ALU.subtract)
                ins.then_inc(S["v_lo"], 1)

            def sums(g, u):
                dve.wait_ge(S["exp_ready"], g + 1)
                nc.vector.reduce_sum(ssum[:, :], sc[u][:, :].rearrange("p (w k) -> p w k", k=WIN), AX)\
                    .then_inc(S["sum_ready"], 1)
                dve.wait_ge(S["sum_ready"], g + 1)
                nc.vector.reciprocal(srec[:, :], ssum[:, :]).then_inc(S["rec_ready"], 1)

            def qk_low(g, u):
                dve.wait_ge(S["k_hi"], g + 1)
                nc.vector.scalar_tensor_tensor(k_l[:, :], ps_k, bias_k[:, :], k_h[:, :], ALU.add,
                                               ALU.subtract).then_inc(S["k_lo"], 1)
                dve.wait_ge(S["q_hi"], g + 1)
                nc.vector.scalar_tensor_tensor(q_s[C:P, :], ps_q[C:P], bias_q[C:P, :], q_s[C:P, :], ALU.add,
                                               ALU.subtract).then_inc(S["q_lo"], 1)

            def spread(g, u):
                dve.wait_ge(S["q_lo"], g + 1)
                if past(g, 2):
                    dve.wait_ge(S["s_done"], g - 1)
                q3 = q_s[:, :].rearrange("p (w q) -> p w q", q=WIN)
                for h in range(ACT_HEADS, NH):
                    ins = nc.vector.tensor_scalar(qx[u][:, :, h, :], q3, head_m[:, h:h + 1], None, ALU.mult)
                ins.then_inc(S["qx_dve"], 1)

            def turn(g, u):
                dve.wait_ge(S["norm_ready"], g + 1)
                nc.vector.transpose(prt[:, :], sc[u][:, :]).then_inc(S["pt_ready"], 1)

            def o_low(g, u):
                dve.wait_ge(S["o_hi"], g * 2 + 2)
                for ip in range(2):
                    nc.vector.tensor_tensor(o_dst(o_l, g, ip), o_src(u, ip), o_dst(o_h, g, ip),
                                            ALU.subtract).then_inc(S["o_lo"], 1)

            def pairs(g, u):
                dve.wait_ge(S["pt_lo"], g + 1)
                dve.wait_ge(S["pt_hi"], g + 1)
                if past(g, 2):
                    dve.wait_ge(S["o_done"], g - 1)
                for src, dst in ((pt_h, px_h[u]), (pt_l, px_l[u])):
                    for w in range(2):
                        ins = nc.vector.tensor_scalar(dst[:, :, :, w, :].rearrange("p n a q -> p (n a) q"),
                                                      src[:, :].rearrange("p (n q) -> p n q", q=WIN),
                                                      pair_m[:, w:w + 1], None, ALU.mult)
                ins.then_inc(S["px_ready"], 1)
            attn_steps([(scores, 2), (replicate, 1), (v_low, 2), (sums, 2), (qk_low, 1), (spread, 1), (turn, 2),
                        (o_low, 3), (pairs, 2)], dve.Fori)

            dve.wait_ge(S["vb_ready"], 1)

            def ln1(r, u, w, nt):
                dve.wait_ge(S["h_done"], r + 1)
                n = min(w, P if w == P else TAIL)
                src = ps_h[u][0:n, 0:nt * C].rearrange("p (t c) -> p t c", c=C)
                rows = h2[u][0:w, 0:nt, :]
                if w != P:
                    nc.vector.tensor_copy(rows[n:w], res_t[n:w, :, :]).then_inc(S["cls_in"], 1)
                    dve.wait_ge(S["cls_in"], 1)
                nc.vector.tensor_tensor(rows[0:n], src, b2_bc[0:n, None, :].broadcast_to([n, nt, C]),
                                        ALU.add).then_inc(S["h_ready"], 1)
                dve.wait_ge(S["h_ready"], r + 1)
                if past(r, 1):
                    dve.wait_ge(S["lmean"], r)
                ln_dve_sum(dve, rows, w, nt)
                if past(r, 1):
                    dve.wait_ge(S["lrstd"], r)
                ln_dve_var(dve, r + 1, w, nt)
            blocks_of(dve, ln1)

            dve.wait_ge(S["fw_load"], 6 * 16)
            prep = Step(dve, "fw_prep")
            for out_, in_ in ((w1_h[:, :], w1_f), (f2_h[:, :, :].rearrange("p a c -> p (a c)"), f2_f),
                              (fb2_sb[0:1, :], fb2_f[0:1, :]), (fb2_sb[32:33, :], fb2_f[32:33, :])):
                if out_ is not None:
                    prep.do(nc.vector.tensor_copy(out_, in_))
            prep.do(nc.vector.memset(w1_l[C:P, :], 0.0))
            prep.done()
            for r in (64, 96):
                prep.do(nc.vector.tensor_copy(w1_l[r:r + 1, :], fb1_f[r:r + 1, :]))
            prep.done()
            prep.do(nc.vector.tensor_tensor(w1_l[96:97, :], fb1_f[96:97, :], w1_l[96:97, :], ALU.subtract))
            prep.do(nc.vector.tensor_tensor(w1_l[0:C, :], w1_f[0:C, :], w1_h[0:C, :], ALU.subtract))
            prep.do(nc.vector.tensor_tensor(f2_l[:, :, :].rearrange("p a c -> p (a c)"), f2_f,
                                            f2_h[:, :, :].rearrange("p a c -> p (a c)"), ALU.subtract))
            prep.do(nc.vector.tensor_tensor(fb2_sb[32:33, :], fb2_f[32:33, :], fb2_sb[32:33, :], ALU.subtract))
            prep.done()

            mix = Chain(dve, "dstep", 3)
            for b in range(B):
                mix.start(b)
                if b == 0:
                    dve.wait_ge(S["g_done"], G1 + 1)
                else:
                    dve.wait_ge(S["mA"], 5 * b)
                mix.do(nc.vector.tensor_copy(gram[:, :], ps_g[b]))
                mix.do(nc.vector.tensor_tensor(gcol[:, 0:C], gram[:, 0:C], gram[:, C:P], ALU.add))
                nc.vector.tensor_copy(gcol[:, C:C + 1], gram[:, P:P + 1]).then_inc(S["mB"], 1)
                for n, (dst, src) in enumerate(((grow[0:1, 0:C], bank(0)[0:1, 0:C]), (t1[:, :], bank(1)[0:C + 1, 0:C]),
                                                (ft[:, :], bank(0)[0:C, 0:C]), (fw[:, :], bank(1)[0:C, 0:C]))):
                    dve.wait_ge(S["mA"], 5 * b + n + 1)
                    if n == 1:
                        nc.vector.tensor_scalar(dst, src, 1.0 / SEQ, None, ALU.mult).then_inc(S["mB"], 1)
                    else:
                        nc.vector.tensor_copy(dst, src).then_inc(S["mB"], 1)
                dve.wait_ge(S["mA"], 5 * b + 5)
                nc.vector.tensor_tensor(cvec[:, b, :], bank(1)[:, 0:C], wb_bc[:, :], ALU.add).then_inc(S["mB"], 1)
                mix.do(nc.vector.tensor_tensor(mp_f[:, :], bank(0)[:, 0:C], id2[:, :], ALU.add))
                nc.vector.tensor_copy(mp_h[:, b, :], mp_f[:, :]).then_inc(S["mp_hi"], 1)
                dve.wait_ge(S["mp_hi"], b + 1)
                nc.vector.tensor_tensor(mp_l[:, b, :], mp_f[:, :], mp_h[:, b, :], ALU.subtract).then_inc(S["mB"], 1)

            def mixed(r, u, w, nt):
                dve.wait_ge(S["y_done"], r + 1)
                dve.wait_ge(S["cadd"], B * (NB + 1))
                if past(r, 2):
                    dve.wait_ge(S["acc_ready"], (r - 1) * E)
                src = ps_y[0:w, 0:nt * C].rearrange("p (t c) -> p t c", c=C)
                rows = res[:, bass.ds(r * NT, NT), :] if w == P else res_t[0:w, 0:nt, :]
                nc.vector.tensor_tensor(h2[u][0:w, 0:nt, :], src, rows, ALU.add).then_inc(S["y_ready"], 1)
                dve.wait_ge(S["y_ready"], r + 1)
                dve.wait_ge(S["lmean"], r + G1 + 1)
                ln_dve_sum(dve, h2[u][0:w, 0:nt, :], w, nt)

            def variance(r, u, w, nt):
                dve.wait_ge(S["lrstd"], r + G1 + 1)
                ln_dve_var(dve, r + (G1 + 2), w, nt)

            top = Chain(dve, "gstep", 8)

            def select(r, u, w, nt):
                top.start(r)
                dve.wait_ge(S["gate_done"], r + 1)
                g3 = gs[0:w, 0:nt, :]
                nc.vector.tensor_tensor(g3, ps_gate[0:w, 0:nt * E].rearrange("p (t e) -> p t e", e=E),
                                        bg_bc[0:w, None, :].broadcast_to([w, nt, E]), ALU.add).then_inc(S["gate_ready"], 1)
                dve.wait_ge(S["gate_ready"], r + 1)
                other = g3[:, :, None, :].broadcast_to([w, nt, E, E])
                own = g3[:, :, :, None].broadcast_to([w, nt, E, E])
                c4 = gcmp[0:w, 0:nt, :].rearrange("p t (e j) -> p t e j", j=E)
                q4 = geq[0:w, 0:nt, :].rearrange("p t (e j) -> p t e j", j=E)
                top.do(nc.vector.tensor_tensor(q4, other, own, ALU.is_equal))
                top.do(nc.vector.tensor_tensor(geq[0:w, 0:nt, :], geq[0:w, 0:nt, :],
                                               low_m[0:w, None, :].broadcast_to([w, nt, E * E]), ALU.mult))
                top.do(nc.vector.tensor_tensor(c4, other, own, ALU.is_gt))
                top.do(nc.vector.tensor_tensor(gcmp[0:w, 0:nt, :], gcmp[0:w, 0:nt, :], geq[0:w, 0:nt, :], ALU.add))
                top.do(nc.vector.reduce_sum(gcnt[0:w, 0:nt * E], gcmp[0:w, 0:nt, :].rearrange("p t (e j) -> p (t e) j", j=E), AX))
                top.do(nc.vector.reduce_max(gmx[0:w, 0:nt], g3, AX))
                nc.vector.tensor_tensor(gex[0:w, 0:nt, :], g3, gmx[0:w, 0:nt, None].broadcast_to([w, nt, E]),
                                        ALU.subtract).then_inc(S["selected"], 1)

            def weigh(r, u, w, nt):
                dve.wait_ge(S["gexp"], r + 1)
                c3 = gcnt[0:w, 0:nt * E].rearrange("p (t e) -> p t e", e=E)
                nc.vector.scalar_tensor_tensor(gex[0:w, 0:nt, :], c3, 2.0, gex[0:w, 0:nt, :], ALU.is_lt,
                                               ALU.mult).then_inc(S["gsel"], 1)
                dve.wait_ge(S["gsel"], r + 1)
                top.do(nc.vector.reduce_sum(gsum[0:w, 0:nt], gex[0:w, 0:nt, :], AX))
                top.do(nc.vector.reciprocal(grec[0:w, 0:nt], gsum[0:w, 0:nt]))
                if past(r, 2):
                    dve.wait_ge(S["yc_ready"], (r - 1) * E)
                nc.vector.tensor_tensor(comb[u][0:w, 0:nt, :], gex[0:w, 0:nt, :],
                                        grec[0:w, 0:nt, None].broadcast_to([w, nt, E]), ALU.mult).then_inc(S["comb_ready"], 1)

            def expert(e, r, u, w, nt):
                n = w * nt
                if e < E:
                    k = r * E + e
                    dve.wait_ge(S["h_hi"], k + 1)
                    if past(r, 1) or e >= 2:
                        dve.wait_ge(S["e_done"], k - 1)
                    nc.vector.scalar_tensor_tensor(hl[e % 2][:, :, 0:n], z_src(e, n), 0.0, hh[e % 2][:, :, 0:n], ALU.max,
                                                   ALU.subtract).then_inc(S["h_lo"], 1)
            expert_blocks(dve, [(1, mixed), (3, variance), (8, select), (8, weigh)], expert)

        @block.tensor
        def _(pe):
            pe.wait_ge(S["split"], 1)
            pe.wait_ge(S["zeros"], 17)
            nc.tensor.matmul(bank(7)[:, 0:C], bias_v[:, :], w2_f, start=True, stop=True).then_inc(S["vb_done"], 1)

            def qk(g, u):
                pe.wait_ge(S["xs_lo"], g * 2 + 2)
                if past(g, 1):
                    pe.wait_ge(S["q_lo"], g)
                nc.tensor.matmul(ps_k, wk_h, xs[u][:, :], start=True, stop=False)
                nc.tensor.matmul(ps_k, wk_l, xs[u][:, :], start=False, stop=True)
                nc.tensor.matmul(ps_q, wq_h, xs[u][:, :], start=True, stop=False)
                nc.tensor.matmul(ps_q, wq_l, xs[u][:, :], start=False, stop=True).then_inc(S["qk_done"], 1)

            def v(g, u):
                pe.wait_ge(S["xrep_ready"], g + 1)
                if past(g, 1):
                    pe.wait_ge(S["v_lo"], g)
                for n in range(NP):
                    toks = xrep[:, n, :, :].rearrange("p a b -> p (a b)")
                    nc.tensor.matmul(ps_v[:, n * C:n * C + C], toks, wv_h, start=True, stop=False)
                    ins = nc.tensor.matmul(ps_v[:, n * C:n * C + C], toks, wv_l, start=False, stop=True)
                ins.then_inc(S["v_done"], 1)

            def s(g, u):
                pe.wait_ge(S["qx_dve"], g + 1)
                pe.wait_ge(S["qx_act"], g + 1)
                pe.wait_ge(S["k_lo"], g + 1)
                if past(g, 2):
                    pe.wait_ge(S["sc_ready"], g - 1)
                for w in range(NW):
                    q = qx[u][:, w, :, :].rearrange("p h q -> p (h q)")
                    cols = slice(w * WIN, (w + 1) * WIN)
                    nc.tensor.matmul(ps_s[u][:, cols], q, k_h[:, cols], start=True, stop=False)
                    ins = nc.tensor.matmul(ps_s[u][:, cols], q, k_l[:, cols], start=False, stop=True)
                ins.then_inc(S["s_done"], 1)

            def av(g, u):
                pe.wait_ge(S["px_ready"], g + 1)
                pe.wait_ge(S["v_lo"], g + 1)
                if past(g, 2):
                    pe.wait_ge(S["o_lo"], g * 2 - 2)
                for n in range(NP):
                    dst = ps_o[u][:, n * 2 * WIN:(n + 1) * 2 * WIN]
                    k = 0
                    for a in range(2):
                        for px in (px_h[u], px_l[u]):
                            ins = nc.tensor.matmul(dst, vx[u][:, n, a, :], px[:, n, a, :, :].rearrange("p w q -> p (w q)"),
                                                   start=k == 0, stop=k == 3)
                            k += 1
                ins.then_inc(S["o_done"], 1)
            attn_steps([(s, 2), (v, 2), (qk, 1), (av, 3)], pe.Fori)

            pe.wait_ge(S["o_lo"], 2 * AB)
            pe.wait_ge(S["o_hi"], 2 * AB)
            for b in range(B):
                nc.tensor.matmul(ps_g[b], x1t_t[:, B * TW:B * TW + P], wpk_h[:, 0:P + 1], start=True, stop=False,
                                 skip_group_check=True)

            def project(r, u, w, nt):
                if past(r, 2):
                    pe.wait_ge(S["h_ready"], r - 1)
                n = P if w == P else TAIL
                for t in range(nt):
                    first = r * T + r // NB * TAIL + t * P if w == P else t * TOK + NB * T
                    cols = bass.ds(first, n)
                    dst = ps_h[u][0:n, t * C:(t + 1) * C]
                    nc.tensor.matmul(dst, o_h[:, cols], w2_h, start=True, stop=False)
                    nc.tensor.matmul(dst, o_h[:, cols], w2_l, start=False, stop=False)
                    ins = nc.tensor.matmul(dst, o_l[:, cols], w2_h, start=False, stop=True)
                ins.then_inc(S["h_done"], 1)

            def turn_gram(r, u, w, nt, b):
                pe.wait_ge(S["llo"], r + 1)
                if past(r, 2):
                    pe.wait_ge(S["t_copied"], r - 1)
                for t in range(nt):
                    ins = nc.tensor.transpose(ps_t1(u)[:, t * P:t * P + w], xt[u][0:w, t, 0:P], id_h[0:w, 0:w])
                ins.then_inc(S["t_done"], 1)
                for t in range(nt):
                    ins = nc.tensor.matmul(ps_g[t if b is None else b], xt[u][0:w, t, 0:P], xt[u][0:w, t, 0:P + 1],
                                           start=False, stop=b is None, skip_group_check=True)
                ins.then_inc(S["g_done"], 1)

            project(0, 0, P, NT)
            for b in range(B):
                if b == 0:
                    for u in range(2):
                        project(u + 1, 1 - u, P, NT)
                        turn_gram(u, u, P, NT, b)
                with pe.Fori(int(b == 0), NB // 2 - (b == B - 1)) as i:
                    for u in range(2):
                        r = i * 2 + (b * NB + u)
                        project(r + 1, 1 - u, P, NT)
                        turn_gram(r, u, P, NT, b)
            project(G1 - 1, 1, P, NT)
            turn_gram(G1 - 2, 0, P, NT, B - 1)
            project(G1, 0, TW, B)
            turn_gram(G1 - 1, 1, P, NT, B - 1)
            turn_gram(G1, 0, TW, B, None)

            for b in range(B):
                mB = MB * b
                pe.wait_ge(S["mB"], mB + 1)
                nc.tensor.matmul(bank(0)[0:1, 0:C], gcol[:, C:C + 1], id2[:, :], start=True, stop=True).then_inc(S["mA"], 1)
                pe.wait_ge(S["mB"], mB + 2)
                nc.tensor.matmul(bank(1)[0:C + 1, 0:C], gcol[:, :], gw_sb[:, :], start=True, stop=False)
                nc.tensor.matmul(bank(1)[0:C + 1, 0:C], grow[0:1, :], gb_sb[0:1, :], start=False, stop=True).then_inc(S["mA"], 1)
                pe.wait_ge(S["mB"], mB + 3)
                nc.tensor.matmul(bank(0)[0:C, 0:C], t1[:, :], th_sb[:, :], start=True, stop=True).then_inc(S["mA"], 1)
                pe.wait_ge(S["mB"], mB + 4)
                nc.tensor.matmul(bank(1)[0:C, 0:C], ft[:, :], ww_sb[:, :], start=True, stop=True).then_inc(S["mA"], 1)
                pe.wait_ge(S["mB"], mB + 5)
                nc.tensor.matmul(bank(0)[:, 0:C], ph_sb[:, :], fw[:, :], start=True, stop=True)
                nc.tensor.matmul(bank(1)[:, 0:C], phb_sb[:, :], fw[:, :], start=True, stop=True).then_inc(S["mA"], 1)
            pe.wait_ge(S["mB"], MB * B)
            pe.wait_ge(S["t_copied"], G1 + 1)
            pe.wait_ge(S["fw_prep"], 11)

            def mix(r, u, w, nt):
                if past(r, 1):
                    pe.wait_ge(S["gate_ready"], r)
                for t in range(nt):
                    if w == P:
                        toks = x1t[:, bass.ds(r, 1), t * P:(t + 1) * P].rearrange("p a b -> p (a b)")
                        m_h, m_l = (m[:, bass.ds(r // NB, 1), :].rearrange("p a c -> p (a c)") for m in (mp_h, mp_l))
                    else:
                        toks = x1t_t[:, t * TW:(t + 1) * TW]
                        m_h, m_l = mp_h[:, t, :], mp_l[:, t, :]
                    dst = ps_y[0:w, t * C:(t + 1) * C]
                    nc.tensor.matmul(dst, toks, m_h, start=True, stop=False)
                    ins = nc.tensor.matmul(dst, toks, m_l, start=False, stop=True)
                ins.then_inc(S["y_done"], 1)

            def turn(r, u, w, nt):
                pe.wait_ge(S["llo"], r + (G1 + 2))
                if past(r, 1):
                    pe.wait_ge(S["xb_ready"], r)
                for t in range(nt):
                    ins = nc.tensor.transpose(ps_t2[:, t * P:t * P + w], xt[u][0:w, t, 0:P], id_h[0:w, 0:w])
                ins.then_inc(S["t_done"], 1)

            def gate(r, u, w, nt):
                pe.wait_ge(S["xa_ready"], r + 1)
                pe.wait_ge(S["y_ready"], r + 1)
                for t in range(nt):
                    toks = xa[u][:, t * w:t * w + w]
                    dst = ps_gate[0:w, t * E:(t + 1) * E]
                    nc.tensor.matmul(dst, toks, wg_h, start=True, stop=False)
                    ins = nc.tensor.matmul(dst, toks, wg_l, start=False, stop=True)
                ins.then_inc(S["gate_done"], 1)

            def expert(e, r, u, w, nt):
                n = w * nt
                if e < E:
                    k = r * E + e
                    if e == 0:
                        pe.wait_ge(S["xb_ready"], r + 1)
                    if past(r, 1) or e >= 2:
                        pe.wait_ge(S["h_lo"], k - 1)
                    for m in range(NM):
                        cols = slice((e * NM + m) * P, (e * NM + m + 1) * P)
                        dst = bank(2 * (e % 2) + m)[:, 0:n]
                        nc.tensor.matmul(dst, w1_h[:, cols], xa[u][:, 0:n], start=True, stop=False)
                        ins = nc.tensor.matmul(dst, w1_l[:, cols], xb[u][:, 0:n], start=False, stop=True)
                    ins.then_inc(S["z_done"], 1)
                if e:
                    f = e - 1
                    k = r * E + f
                    pe.wait_ge(S["h_lo"], k + 1)
                    pe.wait_ge(S["h_hi"], k + 1)
                    if past(r, 1) or f >= 2:
                        pe.wait_ge(S["ye_ready"], k - 1)
                    for t in range(nt):
                        dst = ps_ye[f % 2][:, t * C:(t + 1) * C]
                        nc.tensor.matmul(dst, one_rows[:, :], fb2_sb[:, f * C:(f + 1) * C], start=True, stop=False)
                        for m in range(NM):
                            hi = hh[f % 2][:, m, t * w:t * w + P]
                            lo = hl[f % 2][:, m, t * w:t * w + P]
                            nc.tensor.matmul(dst, hi, f2_h[:, f * NM + m, :], start=False, stop=False)
                            nc.tensor.matmul(dst, hi, f2_l[:, f * NM + m, :], start=False, stop=False)
                            ins = nc.tensor.matmul(dst, lo, f2_h[:, f * NM + m, :], start=False, stop=m == NM - 1)
                    ins.then_inc(S["e_done"], 1)
            expert_blocks(pe, [(1, mix), (5, turn), (7, gate)], expert)


def _f(a):
    return np.ascontiguousarray(a)


def kernel(**inputs):
    import concourse.bacc as bacc
    from concourse.bass_utils import run_bass_kernel_spmd

    v = {n: np.asarray(a) for n, a in inputs.items()}
    order = [(hp, a, e) for a in range(2) for hp in range(NH // 2) for e in range(HE)]
    v_of = np.array([e * NH + 2 * hp + a for hp, a, e in order])
    o_of = np.array([(2 * hp + a) * HE + e for hp, a, e in order])
    w1 = v["L0_tok_w1"].reshape(C, 3, C)
    b1 = v["L0_tok_b1"].reshape(C, 3)
    at = np.array([[i, j] for i in range(WS) for j in range(WS)])
    rel = at[None, :, :] - at[:, None, :] + WS - 1
    q, k = np.arange(WIN)[:, None], np.arange(WIN)[None, :]
    row = np.where((q // WS < WS // 2) != (k // WS < WS // 2), MASKED, 0.0)
    col = np.where((q % WS < WS // 2) != (k % WS < WS // 2), MASKED, 0.0)
    masks = np.zeros((WIN, 3 * WROW, WIN), np.float32)
    masks[:, 2 * WROW:, :] += row[:, None, :]
    masks[:, WROW - 1::WROW, :] += col[:, None, :]
    part = np.arange(P)
    chan = np.arange(C)

    def rows(a, n=P):
        return _f(np.broadcast_to(a.reshape(1, -1), (n, a.size)))

    arrays = {
        "x": v["x"],
        "wq": np.tile(w1[:, 0].T, (2, 2)), "wk": np.tile(w1[:, 1].T, (2, 2)), "wv": np.tile(w1[v_of, 2].T, (2, 1)),
        "bq": np.tile(b1[:, 0:1], (2, 1)), "bk": np.tile(b1[:, 1:2], (2, 1)),
        "bv": np.broadcast_to(np.concatenate([b1[v_of, 2:3], np.zeros((C, 1), np.float32)]), (P, P)),
        "w2": np.tile(v["L0_tok_w2"].T[o_of], (2, 1)), "b2": rows(v["L0_tok_b2"]),
        "pos": np.tile(v["L0_tok_pos_emb"][rel[..., 0], rel[..., 1]], (NH, 1)),
        "wmask": np.tile(masks.reshape(WIN, -1), (NH, 1)),
        "pairmask": (part[:, None] // WIN % 2 == np.arange(2)[None, :]).astype(np.float32),
        "headmask": (part[:, None] % NH == np.arange(NH)[None, :]).astype(np.float32),
        "ident": np.eye(P, dtype=np.float16), "ident2": np.tile(np.eye(C, dtype=np.float32), (2, 1)),
        "cls": np.broadcast_to(v["cls_tok"], (1, B, C)),
        "gw": np.tile(v["L0_attn_g_w"].T, (2, 1)), "gb": v["L0_attn_g_b"].reshape(1, C),
        "thw": np.concatenate([v["L0_attn_theta_w"].T, v["L0_attn_theta_b"].reshape(1, C)]),
        "phw": np.tile(v["L0_attn_phi_w"], (1, 2)), "phb": np.broadcast_to(v["L0_attn_phi_b"][:, None], (C, P)),
        "ww": v["L0_attn_W_w"].T, "wb": rows(v["L0_attn_W_b"]),
        "wg": np.tile(v["L0_ffn_Wg"].T, (2, 1)), "bg": rows(v["L0_ffn_bg"]),
        "f1": np.tile(v["L0_ffn_W1"].transpose(2, 0, 1).reshape(C, E * HID), (2, 1)),
        "fb1": v["L0_ffn_b1"].reshape(1, E * HID),
        "f2": v["L0_ffn_W2"].reshape(E, C, NM, P).transpose(3, 0, 2, 1).reshape(P, E * NM * C),
        "fb2": v["L0_ffn_b2"].reshape(1, E * C),
        "lower": rows((chan % E < chan // E).astype(np.float32)),
    }
    nc = bacc.Bacc("TRN2", target_bir_lowering=False, num_devices=1)
    arrays = {f"in_{n}": _f(a) for n, a in arrays.items()}
    args = {n[3:]: nc.dram_tensor(n, a.shape, mybir.dt.from_np(a.dtype), kind="ExternalInput").ap()
            for n, a in arrays.items()}
    out = nc.dram_tensor("out_dram", (B * SEQ, C), F32, kind="ExternalOutput").ap()
    swin_linattn_moe(nc, out=out, **args)
    r = run_bass_kernel_spmd(nc, [arrays], core_ids=[0])
    return r.results[0]["out_dram"].reshape(B, SEQ, C)
```

```python
from contextlib import ExitStack

import numpy as np

import concourse.bass as bass
from concourse import mybir

P = 128
F32 = mybir.dt.float32
F16 = mybir.dt.float16
ALU = mybir.AluOpType
ACT = mybir.ActivationFunctionType
AX = mybir.AxisListType.X

B, C, HT, WD = 4, 64, 56, 56
WS, NH, HE = 4, 8, 8
WIN = WS * WS
WROW = WD // WS
TOK = HT * WD
SEQ = TOK + 1
NW = 2 * WROW
NP = NW // 2
AT = NW * WIN
AB = B * (HT // WS) // 2
ABB = AB // B
T = 512
NT = T // P
NB = TOK // T
TAIL = TOK - NB * T
TW = TAIL + 1
E, HID = 8, 256
NM = HID // P
G1 = B * NB
CH = E * NM
LAG = 3
EPS = 1e-5
SCALE = 1.0 / float(np.sqrt(np.float32(C / NH)))
MASKED = -1e30
TINY = 1e-37


def swin_linattn_moe(nc, x, wq, wk, wv, bq, bk, bv, w2, b2, pos, wmask, pairmask, headmask, ident, ident2,
                     cls, gw, gb, thw, phw, phb, ww, wb, wg, bg, f1, fb1, f2, fb2, lower, out):
    ctx = ExitStack()
    with ctx:
        def sb(name, shape, dt=F32):
            return ctx.enter_context(nc.sbuf_tensor(name, shape, dt))

        def sem(name):
            return ctx.enter_context(nc.semaphore(name))

        wst = sb("weights_f32", [P, 3 * P + 3 * C])
        wq_f, wk_f = wst[:, 0:P], wst[:, P:2 * P]
        wv_f, w2_f = wst[:, 2 * P:2 * P + C], wst[:, 2 * P + C:3 * P]
        wpk_h = sb("weights_h", [P, 3 * P + E], F16)
        wpk_l = sb("weights_l", [P, 3 * P + E], F16)
        wq_h, wk_h, wv_h, w2_h = wpk_h[:, 0:P], wpk_h[:, P:2 * P], wpk_h[:, 2 * P:2 * P + C], wpk_h[:, 2 * P + C:3 * P]
        wq_l, wk_l, wv_l, w2_l = wpk_l[:, 0:P], wpk_l[:, P:2 * P], wpk_l[:, 2 * P:2 * P + C], wpk_l[:, 2 * P + C:3 * P]
        wg_h, wg_l = wpk_h[:, 3 * P:3 * P + E], wpk_l[:, 3 * P:3 * P + E]
        bias_q, bias_k, bias_v = sb("bias_q", [P, 1]), sb("bias_k", [P, 1]), sb("bias_v", [P, P])
        b2_bc = sb("b2_bc", [P, C])
        pos_sb = sb("pos_sb", [P, WIN])
        score_bias = sb("score_bias", [P, 3 * WROW, WIN])
        pair_m = sb("pair_m", [P, 2])
        head_m = sb("head_m", [P, NH])
        id_h = sb("id_h", [P, P], F16)
        id2 = sb("id2", [P, C])
        gw_sb, gb_sb = sb("gw_sb", [P, C]), sb("gb_sb", [1, C])
        th_sb, ph_sb, phb_sb = sb("th_sb", [C + 1, C]), sb("ph_sb", [C, P]), sb("phb_sb", [C, P])
        ww_sb, wb_bc = sb("ww_sb", [C, C]), sb("wb_bc", [P, C])
        bg_bc = sb("bg_bc", [P, E])
        low_m = sb("low_m", [P, E * E])
        half_neg = sb("half_neg", [P, NT])
        w1_h = sb("w1_h", [P, E * HID], F16)
        w1_l = sb("w1_l", [P, E * HID], F16)
        f2_h = sb("f2_h", [P, E * NM, C], F16)
        f2_l = sb("f2_l", [P, E * NM, C], F16)
        fb2_sb = sb("fb2_sb", [P, E * C], F16)
        one_rows = sb("one_rows", [P, P], F16)
        img = sb("img", [P, 2 * HT, WD])
        xs = [sb(f"xs{i}", [P, AT], F16) for i in range(4)]
        xrep = sb("xrep", [P, NP, 4, 2 * WIN], F16)
        k_h, k_l = sb("k_h", [P, AT], F16), sb("k_l", [P, AT], F16)
        q_s = sb("q_s", [P, AT], F16)
        spread_buf = sb("spread_buf", [P, 4, NW * P], F16)
        qx = [spread_buf[:, i, :].rearrange("p (w h q) -> p w h q", h=NH, q=WIN) for i in range(2)]
        sc = [sb(f"sc{i}", [P, AT]) for i in range(2)]
        smax, ssum, srec = ([sb(f"{n}{i}", [P, NW]) for i in range(2)] for n in ("smax", "ssum", "srec"))
        prt = sb("prt", [P, AT])
        pt = sb("pt", [P, 2, AT], F16)
        pt_h, pt_l = pt[:, 0, :], pt[:, 1, :]
        px = [sb(f"px{i}", [P, 2, NP, 2, 2, WIN], F16) for i in range(2)]
        vx = [spread_buf[:, 2 + i, :].rearrange("p (n a c) -> p n a c", a=2, c=P) for i in range(2)]
        o_h = sb("o_h", [P, B * TOK], F16)
        o_l = sb("o_l", [P, B * TOK], F16)
        res = sb("res", [P, B * NB * NT, C])
        res_t = sb("res_t", [P, B, C])
        x1t = spread_buf[:, :, :].rearrange("p i n -> p (i n)")[:, 0:B * NB * T].rearrange("p (r n) -> p r n", n=T)
        x1t_t = sb("x1t_t", [P, B * TW + P], F16)
        xt = [sb(f"xt{i}", [P, NT, P + 2], F16) for i in range(2)]
        ln_s, pad = sb("ln_s", [P, NT, 6]), sb("pad", [P, 1])
        ln_m = [sb(f"ln_m{i}", [P, NT, 2]) for i in range(2)]
        ln_v = [sb(f"ln_v{i}", [P, NT]) for i in range(2)]
        ln_r = [sb(f"ln_r{i}", [P, NT]) for i in range(2)]
        ln_n = [sb(f"ln_n{i}", [P, NT, C]) for i in range(2)]
        gram = sb("gram", [P, P + 1])
        gcol = sb("gcol", [P, C + 1])
        grow = sb("grow", [1, C + 1])
        t1, ft, fw = sb("t1", [C + 1, C]), sb("ft", [C, C]), sb("fw", [C, C])
        mp_f = sb("mp_f", [P, C])
        mp_h, mp_l = sb("mp_h", [P, B, C], F16), sb("mp_l", [P, B, C], F16)
        cvec = sb("cvec", [P, B, C])
        h2 = [sb(f"h2{i}", [P, NT, C]) for i in range(2)]
        xa = [sb(f"xa{i}", [P, T], F16) for i in range(2)]
        xb = [sb(f"xb{i}", [P, T], F16) for i in range(2)]
        gs = sb("gs", [P, NT, E])
        gcmp = sb("gcmp", [P, NT, E * E])
        gcnt, gmx, gex = sb("gcnt", [P, NT * E]), sb("gmx", [P, NT]), sb("gex", [P, NT, E])
        gsum, grec = sb("gsum", [P, NT]), sb("grec", [P, NT])
        comb = [sb(f"comb{i}", [P, NT, E]) for i in range(2)]
        hh = [sb(f"hh{i}", [P, NM, T], F16) for i in range(2)]
        hl = [sb(f"hl{i}", [P, NM, T], F16) for i in range(2)]
        ye = [sb(f"ye{i}", [P, NT, C]) for i in range(2)]
        yc = sb("yc", [P, NT, C])
        acc = [sb(f"acc{i}", [P, NT, C]) for i in range(2)]
        flat = img[:, :, :].rearrange("p a b -> p (a b)")
        w1_f = flat[:, 0:E * HID]
        f2_f = flat[:, E * HID:E * HID + E * NM * C]
        fb1_f = flat[:, HT * WD:HT * WD + E * HID]
        fb2_f = flat[:, HT * WD + E * HID:HT * WD + E * HID + E * C]

        ps = ctx.enter_context(nc.psum_tensor("ps", [P, 8 * 512], F32))

        def bank(i, n=1):
            return ps[:, 512 * i:512 * (i + n)]

        ps_q, ps_k, ps_v = bank(0)[:, 0:AT], bank(1)[:, 0:AT], bank(2, 2)
        ps_s = [bank(4)[:, 0:AT], bank(5)[:, 0:AT]]
        ps_o = [bank(6)[:, 0:AT], bank(7)[:, 0:AT]]
        ps_h = [bank(0), bank(1)]
        ps_g = [bank(4 + b)[:, 0:P + 1] for b in range(B)]
        ps_ye = [bank(4), bank(5)]
        ps_t2 = bank(6).bitcast(F16)[:, 0:NT * P]
        ps_y, ps_gate = bank(7)[:, 0:NT * C], bank(7)[:, NT * C:NT * C + NT * E]
        ACT_HEADS = 5

        def ps_t1(u):
            return bank(2 + u).bitcast(F16)[:, 0:NT * P]

        def z_src(e, m, n):
            return bank(2 * (e % 2) + m)[:, 0:n]

        def y_src(e, w, nt):
            return ps_ye[e % 2][0:w, 0:nt * C].rearrange("p (t c) -> p t c", c=C)

        def v_src(hp):
            return ps_v[32 * hp:32 * hp + 32, 0:NP * C].rearrange("p (n a h e) -> p n a h e", a=2, e=HE, h=NH // 2)[:, :, :, hp, :]

        def v_diag(u, hp, lo):
            base = vx[u][32 * hp:32 * hp + 32]
            return bass.AP(base.tensor, base.offset + lo * C + hp * HE,
                           [list(base.ap[0]), [2 * P, NP], [P + C // 2, 2], [1, HE]])

        def o_src(u, ip):
            return ps_o[u][:, ip * AT // 2:(ip + 1) * AT // 2].rearrange("p (j a b) -> p j a b", a=WS, b=WS)

        def o_dst(buf, g, ip):
            return buf[:, bass.ds(g * AT + ip * AT // 2, AT // 2)].rearrange("p (a j b) -> p j a b", a=WS, b=WS)

        names = ("consts img split img_free xs_ready xs_lo xrep_ready k_hi k_lo q_hi q_lo qx_dve qx_act "
                 "qk_done v_done s_done o_done v_hi v_lo sc_ready max_ready shift_ready exp_ready sum_ready rec_ready "
                 "norm_ready pt_ready pt_hi pt_lo px_ready o_hi o_lo sbias zeros "
                 "h_done h_ready lstats lmean lveps lrstd lnorm lhi llo t_done t_copied g_done "
                 "mA mB dstep y_done y_ready cadd xT_ready xa_ready xb_ready gate_done gate_ready gstep wstep comb_ready selected gsel mp_hi cls_in kept vb_done vb_ready gexp "
                 "z_done h_hi h_lo e_done ye_ready yc_ready acc_ready stored0 stored1 fw_load fw_stage fw_prep acc_init").split()
        S = {n: sem(n) for n in names}
        block = ctx.enter_context(nc.Block())

        class Step:
            def __init__(self, eng, name):
                self.eng, self.name, self.n = eng, name, 0

            def do(self, ins):
                self.n += 1
                ins.then_inc(S[self.name], 1)

            def done(self):
                self.eng.wait_ge(S[self.name], self.n)

        CONSTS = [(wq_f, wq), (wk_f, wk), (wv_f, wv), (w2_f, w2), (wst[:, 3 * P:3 * P + E], wg), (bias_q, bq), (bias_k, bk), (bias_v, bv),
                  (b2_bc, b2), (pos_sb, pos), (pair_m, pairmask), (head_m, headmask), (id_h, ident), (id2, ident2),
                  (score_bias[:, :, :].rearrange("p a b -> p (a b)"), wmask), (gw_sb, gw), (gb_sb, gb), (th_sb, thw),
                  (ph_sb, phw), (phb_sb, phb), (ww_sb, ww), (wb_bc, wb), (bg_bc, bg), (low_m, lower)]
        CONST_WAIT = 16 * len(CONSTS) + 16

        def full(t):
            return t[:, :] if hasattr(t, "shape") and len(t.shape) == 2 else t

        def load_image(eng, b):
            s = WS // 2
            if b:
                eng.wait_ge(S["img"], IMG * b)
            for half in range(2):
                d = img[C * half:C * half + C, HT * (b % 2):HT * (b % 2) + HT, :]
                for (dy, sy, ny) in ((0, s, HT - s), (HT - s, 0, s)):
                    for (dx, sx, nx) in ((0, s, WD - s), (WD - s, 0, s)):
                        eng.dma_start(d[:, dy:dy + ny, dx:dx + nx],
                                      x[b, :, sy:sy + ny, sx:sx + nx]).then_inc(S["img"], 16)

        IMG = 8 * 16

        def attn_steps(stages, loop):
            depth = max(lag for _, lag in stages)
            lead = 8

            def step(s, u, check):
                for fn, lag in stages:
                    if not check or 0 <= s - lag < AB:
                        fn(s - lag, (u - lag) % 4)
            for s in range(lead):
                step(s, s % 4, True)
            trips = (AB - lead) // 4
            with loop(0, trips) as i:
                for u in range(4):
                    step(i * 4 + (lead + u), u, False)
            for s in range(lead + 4 * trips, AB + depth):
                step(s, s % 4, True)

        def past(g, n):
            return not isinstance(g, int) or g >= n

        @block.sync
        def _(sp):
            load_image(sp, 0)
            for dst, src in CONSTS:
                sp.dma_start(full(dst), src).then_inc(S["consts"], 16)
            sp.dma_start(res_t[TAIL:TW, :, :], cls).then_inc(S["consts"], 16)
            load_image(sp, 1)
            for b in range(2, B):
                sp.wait_ge(S["xs_lo"], 2 * ABB * (b - 1))
                load_image(sp, b)
            sp.wait_ge(S["xs_lo"], 2 * AB)
            sp.dma_start(w1_f, f1).then_inc(S["fw_load"], 16)
            sp.dma_start(f2_f, f2).then_inc(S["fw_load"], 16)
            for r in (64, 96):
                sp.dma_start(fb1_f[r:r + 1, :], fb1).then_inc(S["fw_load"], 16)
            for r in (0, 32):
                sp.dma_start(fb2_f[r:r + 1, :], fb2).then_inc(S["fw_load"], 16)

            def store(b, r, u, n):
                sp.wait_ge(S["acc_ready"], n)
                base = b * SEQ + 1 + r * T
                sp.dma_start(out[bass.ds(base, T), :].rearrange("(t p) c -> p t c", p=P),
                             acc[u][:, :, :]).then_inc(S[f"stored{u}"], 16)
            for b in range(B):
                with sp.Fori(0, NB // 2) as i:
                    for u in range(2):
                        r = i * 2 + u
                        store(b, r, u, E * (r + b * NB + 1))
            sp.wait_ge(S["acc_ready"], E * (B * NB + 1))
            for b in range(B):
                sp.dma_start(out[b * SEQ + 1 + NB * T:(b + 1) * SEQ, :], acc[0][0:TAIL, b, :]).then_inc(S["stored0"], 16)
                sp.dma_start(out[b * SEQ:b * SEQ + 1, :], acc[0][TAIL:TW, b, :]).then_inc(S["stored0"], 16)
            sp.wait_ge(S["stored0"], 16 * (G1 // 2 + 2 * B))
            sp.wait_ge(S["stored1"], 16 * (G1 // 2))

        def ln_stats(dve, src, m, u, w, nt):
            for t in range(nt):
                ins = nc.vector.bn_stats(ln_s[0:w, t, :], src[:, t, :])
            ins.then_inc(S["lstats"], 1)
            dve.wait_ge(S["lstats"], m)
            nc.vector.memset(pad[:, :], 0.0)
            for t in range(nt):
                ins = nc.vector.bn_aggr(ln_m[u][0:w, t, :], ln_s[0:w, t, :])
            ins.then_inc(S["lmean"], 1)
            dve.wait_ge(S["lmean"], m)
            nc.vector.tensor_scalar(ln_v[u][0:w, 0:nt], ln_m[u][0:w, 0:nt, 1], EPS, None, ALU.add).then_inc(S["lveps"], 1)

        def ln_rstd(pool, m, u, w, nt):
            pool.wait_ge(S["lveps"], m)
            nc.gpsimd.tensor_tensor(ln_r[u][0:w, 0:nt], ln_v[u][0:w, 0:nt], half_neg[0:w, 0:nt],
                                    ALU.pow).then_inc(S["lrstd"], 1)

        def ln_normalise(dve, src, m, u, w, nt):
            dve.wait_ge(S["lrstd"], m)
            for t in range(nt):
                ins = nc.vector.tensor_scalar(ln_n[u][0:w, t, :], src[:, t, :], ln_m[u][0:w, t, 0:1],
                                              ln_r[u][0:w, t:t + 1], ALU.subtract, ALU.mult)
            ins.then_inc(S["lnorm"], 1)

        def ln_high(act, m, u, w, nt):
            act.wait_ge(S["lnorm"], m)
            nc.scalar.activation(xt[u][0:w, 0:nt, 0:C], ln_n[u][0:w, 0:nt, :], ACT.Copy).then_inc(S["lhi"], 1)

        def ln_low(pool, m, u, w, nt):
            pool.wait_ge(S["lhi"], m)
            nc.gpsimd.tensor_tensor(xt[u][0:w, 0:nt, C:P], ln_n[u][0:w, 0:nt, :], xt[u][0:w, 0:nt, 0:C],
                                    ALU.subtract).then_inc(S["llo"], 1)

        def blocks_of(engine, stages):
            shape = lambda r: (TW, B) if isinstance(r, int) and r == G1 else (P, NT)

            def step(s, u):
                for fn, lag in stages:
                    r = s - lag
                    if not isinstance(r, int) or 0 <= r <= G1:
                        fn(r, (u - lag) % 2, *shape(r))
            for s in range(4):
                step(s, s % 2)
            with engine.Fori(2, G1 // 2) as i:
                for u in range(2):
                    step(i * 2 + u, u)
            for s in range(G1, G1 + 4):
                step(s, s % 2)

        CONST, MIX, MIXED, RSTD, NORMAL, HIGH, LOW, TURN, COLUMNS, GATE, SELECT, GEXP, WEIGH = 0, 0, 2, 3, 5, 6, 7, 9, 10, 11, 13, 16, 18
        MB = 7

        def expert_blocks(engine, prep, body):
            full, tail = (P, NT), (TW, B)

            def one(r, u, shape, ahead):
                for c in range(CH):
                    body(c, r, u, *shape)
                    for at, piece in prep:
                        if at == c and ahead:
                            piece(r + 1, 1 - u, *ahead)
                        if at == c + CH:
                            piece(r, u, *shape)
            for at, piece in prep:
                if at < CH:
                    piece(0, 0, *full)
            for u in range(2):
                one(u, u, full, full)
            with engine.Fori(1, G1 // 2 - 1) as i:
                for u in range(2):
                    one(i * 2 + u, u, full, full)
            one(G1 - 2, 0, full, full)
            one(G1 - 1, 1, full, tail)
            one(G1, 0, tail, None)
            for c in range(CH, CH + LAG):
                body(c, G1, 0, *tail)

        def behind(c, r, u, w, nt):
            c -= LAG
            if c >= 0:
                return c // NM, c % NM, r, u, w, nt
            return (c // NM + E, c % NM, r - 1, 1 - u, P, NT) if past(r, 1) else None

        class Chain:
            def __init__(self, eng, name, per):
                self.eng, self.name, self.per = eng, name, per

            def start(self, r):
                self.r, self.n = r, 0

            def do(self, ins):
                ins.then_inc(S[self.name], 1)
                self.n += 1
                assert self.n <= self.per
                self.eng.wait_ge(S[self.name], self.r * self.per + self.n)

        @block.gpsimd
        def _(pool):
            zeros = Step(pool, "zeros")
            fills = [(vx[0][:, :, :, :], 0.0), (vx[1][:, :, :, :], 0.0), (half_neg[:, :], -0.5), 
                     (one_rows[:, :], 0.0), (fb2_sb[:, :], 0.0), (x1t_t[:, B * TW:B * TW + P], 0.0)]
            fills += [(t[:, :, P:P + 2], 1.0) for t in xt] + [(t[C:P, :], 0.0) for t in xb]
            fills += [(t[r:r + 1, :], 1.0) for t in xb for r in (64, 96)] + [(one_rows[r:r + 1, :], 1.0) for r in (0, 32)]
            for dst, value in fills:
                zeros.do(nc.gpsimd.memset(dst, value))
                zeros.done()

            def take_tokens(g, u):
                pool.wait_ge(S["img"], IMG * (g // ABB + 1))
                if past(g, 4):
                    pool.wait_ge(S["xrep_ready"], g - 3)
                    pool.wait_ge(S["qk_done"], g - 3)
                def rows(p0, ip):
                    return img[p0:P, bass.ds(g % (2 * ABB) * (2 * WS) + ip * WS, WS), :]\
                        .rearrange("c a (j b) -> c j a b", b=WS)

                def dst(p0, ip):
                    return xs[u][p0:P, ip * AT // 2:(ip + 1) * AT // 2]\
                        .rearrange("c (j a b) -> c j a b", a=WS, b=WS)
                for ip in range(2):
                    nc.gpsimd.tensor_copy(dst(0, ip), rows(0, ip)).then_inc(S["xs_ready"], 1)
                pool.wait_ge(S["xs_ready"], g * 2 + 2)
                for ip in range(2):
                    nc.gpsimd.tensor_tensor(dst(C, ip), rows(C, ip), dst(C, ip), ALU.subtract).then_inc(S["xs_lo"], 1)
                pool.wait_ge(S["xs_lo"], g * 2 + 2)

            def shift(g, u):
                pool.wait_ge(S["max_ready"], g + 1)
                s3 = sc[u % 2][:, :].rearrange("p (w k) -> p w k", k=WIN)
                nc.gpsimd.tensor_tensor(s3, s3, smax[u % 2][:, :, None].broadcast_to([P, NW, WIN]),
                                        ALU.subtract).then_inc(S["shift_ready"], 1)

            def normalise(g, u):
                pool.wait_ge(S["rec_ready"], g + 1)
                s3 = sc[u % 2][:, :].rearrange("p (w k) -> p w k", k=WIN)
                nc.gpsimd.tensor_tensor(s3, s3, srec[u % 2][:, :, None].broadcast_to([P, NW, WIN]),
                                        ALU.mult).then_inc(S["norm_ready"], 1)

            def low_part(g, u):
                pool.wait_ge(S["pt_hi"], g + 1)
                if past(g, 1):
                    pool.wait_ge(S["px_ready"], g)
                nc.gpsimd.tensor_tensor(pt_l, prt[:, :], pt_h, ALU.subtract).then_inc(S["pt_lo"], 1)

            attn_steps([(low_part, 5), (normalise, 4), (shift, 3), (take_tokens, 0)], pool.Fori)

            blocks_of(pool, [(lambda r, u, w, nt: ln_rstd(pool, r + 1, u, w, nt), 0),
                             (lambda r, u, w, nt: ln_low(pool, r + 1, u, w, nt), 1)])

            pool.wait_ge(S["kept"], G1 + 1)
            pool.wait_ge(S["mB"], MB * B)

            def constant(r, u, w, nt):
                if w == P:
                    rows = res[:, bass.ds(r * NT, NT), :]
                    row = cvec[:, bass.ds(r // NB, 1), :].broadcast_to([P, NT, C])
                    nc.gpsimd.tensor_tensor(rows, rows, row, ALU.add).then_inc(S["cadd"], 1)
                else:
                    nc.gpsimd.tensor_tensor(res_t[0:w, :, :], res_t[0:w, :, :], cvec[0:w, :, :],
                                            ALU.add).then_inc(S["cadd"], 1)

            def rstd(r, u, w, nt):
                ln_rstd(pool, r + (G1 + 2), u, w, nt)

            def low(r, u, w, nt):
                ln_low(pool, r + (G1 + 2), u, w, nt)

            def combine(r, u, w, nt, e):
                k = r * E + e
                pool.wait_ge(S["ye_ready"], k + 1)
                if e == 0:
                    pool.wait_ge(S["comb_ready"], r + 1)
                if past(k, 1):
                    pool.wait_ge(S["acc_ready"], k)
                nc.gpsimd.tensor_tensor(yc[0:w, 0:nt, :], ye[e % 2][0:w, 0:nt, :],
                                        comb[u][0:w, 0:nt, e:e + 1].broadcast_to([w, nt, C]), ALU.mult).then_inc(S["yc_ready"], 1)
                pool.wait_ge(S["yc_ready"], k + 1)
                if e == 0 and past(r, 2):
                    pool.wait_ge(S[f"stored{u}"], r // 2 * 16)
                first = h2[u][0:w, 0:nt, :] if e == 0 else acc[u][0:w, 0:nt, :]
                nc.gpsimd.tensor_tensor(acc[u][0:w, 0:nt, :], first, yc[0:w, 0:nt, :], ALU.add).then_inc(S["acc_ready"], 1)


            def chunk(c, *block):
                done = behind(c, *block)
                if done and done[1] == NM - 1:
                    combine(*done[2:], done[0])
            expert_blocks(pool, [(CONST, constant), (RSTD, rstd), (LOW, low)], chunk)

        @block.scalar
        def _(act):
            act.wait_ge(S["consts"], CONST_WAIT)
            act.wait_ge(S["zeros"], 2)
            act.wait_ge(S["split"], 1)

            def k_high(g, u):
                act.wait_ge(S["qk_done"], g + 1)
                if past(g, 1):
                    act.wait_ge(S["s_done"], g)
                nc.scalar.activation(k_h[:, :], ps_k, ACT.Identity, bias=bias_k[:, :]).then_inc(S["k_hi"], 1)
                if past(g, 1):
                    act.wait_ge(S["qx_dve"], g)
                nc.scalar.activation(q_s[:, :], ps_q, ACT.Identity, bias=bias_q[:, :]).then_inc(S["q_hi"], 1)

            def spread(g, u):
                act.wait_ge(S["q_lo"], g + 1)
                if past(g, 2):
                    act.wait_ge(S["s_done"], g - 1)
                q3 = q_s[:, :].rearrange("p (w q) -> p w q", q=WIN)
                for h in range(ACT_HEADS):
                    ins = nc.scalar.activation(qx[u % 2][:, :, h, :], q3, ACT.Copy, scale=head_m[:, h:h + 1])
                ins.then_inc(S["qx_act"], 1)

            def v_high(g, u):
                act.wait_ge(S["v_done"], g + 1)
                if past(g, 2):
                    act.wait_ge(S["o_done"], g - 1)
                for hp in range(4):
                    nc.scalar.activation(v_diag(u % 2, hp, 0), v_src(hp), ACT.Copy).then_inc(S["v_hi"], 1)

            def exp(g, u):
                act.wait_ge(S["shift_ready"], g + 1)
                nc.scalar.activation(sc[u % 2][:, :], sc[u % 2][:, :], ACT.Exp).then_inc(S["exp_ready"], 1)

            def p_high(g, u):
                act.wait_ge(S["pt_ready"], g + 1)
                if past(g, 1):
                    act.wait_ge(S["px_ready"], g)
                nc.scalar.activation(pt_h, prt[:, :], ACT.Copy).then_inc(S["pt_hi"], 1)

            def o_high(g, u):
                act.wait_ge(S["o_done"], g + 1)
                for ip in range(2):
                    nc.scalar.activation(o_dst(o_h, g, ip), o_src(u % 2, ip), ACT.Copy).then_inc(S["o_hi"], 1)
            attn_steps([(p_high, 5), (k_high, 2), (v_high, 5), (spread, 2), (exp, 3), (o_high, 6)], act.Fori)

            def keep(r, u, w, nt):
                act.wait_ge(S["h_ready"], r + 1)
                if w == P:
                    ins = nc.scalar.activation(res[:, bass.ds(r * NT, NT), :], h2[u][:, :, :], ACT.Copy)
                else:
                    ins = nc.scalar.activation(res_t[0:TAIL, :, :], h2[u][0:TAIL, :, :], ACT.Copy)
                ins.then_inc(S["kept"], 1)

            def high1(r, u, w, nt):
                if past(r, 2):
                    act.wait_ge(S["g_done"], r - 1)
                ln_high(act, r + 1, u, w, nt)

            def turned1(r, u, w, nt):
                act.wait_ge(S["t_done"], r + 1)
                src = ps_t1(u)
                if w == P:
                    ins = nc.scalar.activation(x1t[:, bass.ds(r, 1), :].rearrange("p a b -> p (a b)"), src, ACT.Copy)
                else:
                    ins = nc.scalar.activation(x1t_t[:, 0:B * TW].rearrange("p (t n) -> p t n", n=TW),
                                               src.rearrange("p (t n) -> p t n", n=P)[:, :, 0:TW], ACT.Copy)
                ins.then_inc(S["t_copied"], 1)
            blocks_of(act, [(turned1, 3), (high1, 1), (keep, 0)])

            def high(r, u, w, nt):
                if past(r, 2):
                    act.wait_ge(S["t_done"], r + G1)
                ln_high(act, r + (G1 + 2), u, w, nt)

            def columns(r, u, w, nt):
                act.wait_ge(S["t_done"], r + (G1 + 2))
                if past(r, 2):
                    act.wait_ge(S["z_done"], (r - 1) * (E * NM))
                    act.wait_ge(S["gate_done"], r - 1)
                src = ps_t2.rearrange("p (t n) -> p t n", n=P)[:, 0:nt, 0:w]
                n = w * nt
                nc.scalar.activation(xa[u][:, 0:n].rearrange("p (t n) -> p t n", n=w), src, ACT.Copy).then_inc(S["xa_ready"], 1)
                nc.scalar.activation(xb[u][0:C, 0:n].rearrange("p (t n) -> p t n", n=w), src[0:C], ACT.Copy).then_inc(S["xb_ready"], 1)

            def gate_exp(r, u, w, nt):
                act.wait_ge(S["selected"], r + 1)
                nc.scalar.activation(gex[0:w, 0:nt, :], gex[0:w, 0:nt, :], ACT.Exp).then_inc(S["gexp"], 1)

            def chunk(c, r, u, w, nt):
                e, m, n = c // NM, c % NM, w * nt
                if e < E:
                    act.wait_ge(S["z_done"], r * CH + (c + 1))
                    nc.scalar.activation(hh[e % 2][:, m, 0:n], z_src(e, m, n), ACT.Relu).then_inc(S["h_hi"], 1)
                done = behind(c, r, u, w, nt)
                if done and done[1] == NM - 1:
                    f, _, q, _, w, nt = done
                    k = q * E + f
                    act.wait_ge(S["e_done"], k + 1)
                    if past(q, 1) or f >= 2:
                        act.wait_ge(S["yc_ready"], k - 1)
                    nc.scalar.activation(ye[f % 2][0:w, 0:nt, :], y_src(f, w, nt), ACT.Copy).then_inc(S["ye_ready"], 1)
            expert_blocks(act, [(HIGH, high), (COLUMNS, columns), (GEXP, gate_exp)], chunk)

        @block.vector
        def _(dve):
            dve.wait_ge(S["consts"], CONST_WAIT)
            steps = Step(dve, "sbias")
            nf = 3 * P + E
            steps.do(nc.vector.tensor_copy(wpk_h[:, 0:nf], wst[:, 0:nf]))
            steps.do(nc.vector.tensor_tensor(score_bias[:, :, :], score_bias[:, :, :],
                                             pos_sb[:, None, :].broadcast_to([P, 3 * WROW, WIN]), ALU.add))
            steps.do(nc.vector.memset(grow[:, C:C + 1], float(SEQ)))
            steps.done()
            nc.vector.tensor_tensor(wpk_l[:, 0:nf], wst[:, 0:nf], wpk_h[:, 0:nf], ALU.subtract).then_inc(S["split"], 1)
            dve.wait_ge(S["zeros"], 2)
            dve.wait_ge(S["vb_done"], 1)
            nc.vector.tensor_tensor(b2_bc[:, :], bank(7)[:, 0:C], b2_bc[:, :], ALU.add).then_inc(S["vb_ready"], 1)

            def scores(g, u):
                dve.wait_ge(S["s_done"], g + 1)
                if past(g, 2):
                    dve.wait_ge(S["pt_ready"], g - 1)
                last = g % ABB // (ABB - 1) * WROW
                nc.vector.scalar_tensor_tensor(
                    sc[u % 2][:, :].rearrange("p (w k) -> p w k", k=WIN), ps_s[u % 2].rearrange("p (w k) -> p w k", k=WIN),
                    SCALE, score_bias[:, bass.ds(last, NW), :], ALU.mult, ALU.add).then_inc(S["sc_ready"], 1)

            def maxima(g, u):
                dve.wait_ge(S["sc_ready"], g + 1)
                nc.vector.reduce_max(smax[u % 2][:, :], sc[u % 2][:, :].rearrange("p (w k) -> p w k", k=WIN), AX)\
                    .then_inc(S["max_ready"], 1)

            def replicate(g, u):
                dve.wait_ge(S["xs_lo"], g * 2 + 2)
                if past(g, 1):
                    dve.wait_ge(S["v_done"], g)
                nc.vector.tensor_copy(xrep[:, :, :, :], xs[u][:, :].rearrange("p (a b) -> p a b", b=2 * WIN)
                                      [:, :, None, :].broadcast_to([P, NP, 4, 2 * WIN])).then_inc(S["xrep_ready"], 1)

            def v_low(g, u):
                for hp in range(4):
                    dve.wait_ge(S["v_hi"], g * 4 + (hp + 1))
                    ins = nc.vector.tensor_tensor(v_diag(u % 2, hp, 1), v_src(hp), v_diag(u % 2, hp, 0), ALU.subtract)
                ins.then_inc(S["v_lo"], 1)

            def sums(g, u):
                dve.wait_ge(S["exp_ready"], g + 1)
                nc.vector.reduce_sum(ssum[u % 2][:, :], sc[u % 2][:, :].rearrange("p (w k) -> p w k", k=WIN), AX)\
                    .then_inc(S["sum_ready"], 1)

            def reciprocals(g, u):
                dve.wait_ge(S["sum_ready"], g + 1)
                nc.vector.reciprocal(srec[u % 2][:, :], ssum[u % 2][:, :]).then_inc(S["rec_ready"], 1)

            def qk_low(g, u):
                dve.wait_ge(S["k_hi"], g + 1)
                nc.vector.scalar_tensor_tensor(k_l[:, :], ps_k, bias_k[:, :], k_h[:, :], ALU.add,
                                               ALU.subtract).then_inc(S["k_lo"], 1)
                dve.wait_ge(S["q_hi"], g + 1)
                nc.vector.scalar_tensor_tensor(q_s[C:P, :], ps_q[C:P], bias_q[C:P, :], q_s[C:P, :], ALU.add,
                                               ALU.subtract).then_inc(S["q_lo"], 1)

            def spread(g, u):
                dve.wait_ge(S["q_lo"], g + 1)
                if past(g, 2):
                    dve.wait_ge(S["s_done"], g - 1)
                q3 = q_s[:, :].rearrange("p (w q) -> p w q", q=WIN)
                for h in range(ACT_HEADS, NH):
                    ins = nc.vector.tensor_scalar(qx[u % 2][:, :, h, :], q3, head_m[:, h:h + 1], None, ALU.mult)
                ins.then_inc(S["qx_dve"], 1)

            def turn(g, u):
                dve.wait_ge(S["norm_ready"], g + 1)
                if past(g, 1):
                    dve.wait_ge(S["pt_lo"], g)
                nc.vector.transpose(prt[:, :], sc[u % 2][:, :]).then_inc(S["pt_ready"], 1)

            def o_low(g, u):
                dve.wait_ge(S["o_hi"], g * 2 + 2)
                for ip in range(2):
                    nc.vector.tensor_tensor(o_dst(o_l, g, ip), o_src(u % 2, ip), o_dst(o_h, g, ip),
                                            ALU.subtract).then_inc(S["o_lo"], 1)

            def pairs(g, u):
                dve.wait_ge(S["pt_lo"], g + 1)
                dve.wait_ge(S["pt_hi"], g + 1)
                if past(g, 2):
                    dve.wait_ge(S["o_done"], g - 1)
                for w in range(2):
                    ins = nc.vector.tensor_scalar(px[u % 2][:, :, :, :, w, :].rearrange("p l n a q -> p (l n a) q"),
                                                  pt[:, :, :].rearrange("p l (n q) -> p (l n) q", q=WIN),
                                                  pair_m[:, w:w + 1], None, ALU.mult)
                ins.then_inc(S["px_ready"], 1)
            attn_steps([(sums, 4), (scores, 3), (reciprocals, 4), (maxima, 3), (qk_low, 2), (pairs, 5),
                        (replicate, 4), (spread, 2), (v_low, 5), (turn, 4), (o_low, 6)], dve.Fori)

            dve.wait_ge(S["vb_ready"], 1)

            def ln1(r, u, w, nt):
                dve.wait_ge(S["h_done"], r + 1)
                if past(r, 2):
                    dve.wait_ge(S["kept"], r - 1)
                    dve.wait_ge(S["lnorm"], r - 1)
                n = min(w, P if w == P else TAIL)
                src = ps_h[u][0:n, 0:nt * C].rearrange("p (t c) -> p t c", c=C)
                rows = h2[u][0:w, 0:nt, :]
                if w != P:
                    nc.vector.tensor_copy(rows[n:w], res_t[n:w, :, :]).then_inc(S["cls_in"], 1)
                    dve.wait_ge(S["cls_in"], 1)
                nc.vector.tensor_tensor(rows[0:n], src, b2_bc[0:n, None, :].broadcast_to([n, nt, C]),
                                        ALU.add).then_inc(S["h_ready"], 1)
                dve.wait_ge(S["h_ready"], r + 1)
                ln_stats(dve, rows, r + 1, u, w, nt)

            def normal1(r, u, w, nt):
                if past(r, 2):
                    dve.wait_ge(S["llo"], r - 1)
                ln_normalise(dve, h2[u][0:w, 0:nt, :], r + 1, u, w, nt)
            blocks_of(dve, [(ln1, 0), (normal1, 1)])

            dve.wait_ge(S["fw_load"], 6 * 16)
            prep = Step(dve, "fw_prep")
            for out_, in_ in ((w1_h[:, :], w1_f), (f2_h[:, :, :].rearrange("p a c -> p (a c)"), f2_f),
                              (fb2_sb[0:1, :], fb2_f[0:1, :]), (fb2_sb[32:33, :], fb2_f[32:33, :])):
                if out_ is not None:
                    prep.do(nc.vector.tensor_copy(out_, in_))
            prep.do(nc.vector.memset(w1_l[C:P, :], 0.0))
            prep.done()
            for r in (64, 96):
                prep.do(nc.vector.tensor_copy(w1_l[r:r + 1, :], fb1_f[r:r + 1, :]))
            prep.done()
            prep.do(nc.vector.tensor_tensor(w1_l[96:97, :], fb1_f[96:97, :], w1_l[96:97, :], ALU.subtract))
            prep.do(nc.vector.tensor_tensor(w1_l[0:C, :], w1_f[0:C, :], w1_h[0:C, :], ALU.subtract))
            prep.do(nc.vector.tensor_tensor(f2_l[:, :, :].rearrange("p a c -> p (a c)"), f2_f,
                                            f2_h[:, :, :].rearrange("p a c -> p (a c)"), ALU.subtract))
            prep.do(nc.vector.tensor_tensor(fb2_sb[32:33, :], fb2_f[32:33, :], fb2_sb[32:33, :], ALU.subtract))
            prep.done()

            mix = Chain(dve, "dstep", 3)
            for b in range(B):
                mix.start(b)
                if b == 0:
                    dve.wait_ge(S["g_done"], G1 + 1)
                else:
                    dve.wait_ge(S["mA"], 5 * b)
                mix.do(nc.vector.tensor_copy(gram[:, :], ps_g[b]))
                mix.do(nc.vector.tensor_tensor(gcol[:, 0:C], gram[:, 0:C], gram[:, C:P], ALU.add))
                nc.vector.tensor_copy(gcol[:, C:C + 1], gram[:, P:P + 1]).then_inc(S["mB"], 1)
                for n, (dst, src) in enumerate(((grow[0:1, 0:C], bank(0)[0:1, 0:C]), (t1[:, :], bank(1)[0:C + 1, 0:C]),
                                                (ft[:, :], bank(0)[0:C, 0:C]), (fw[:, :], bank(1)[0:C, 0:C]))):
                    dve.wait_ge(S["mA"], 5 * b + n + 1)
                    if n == 1:
                        nc.vector.tensor_scalar(dst, src, 1.0 / SEQ, None, ALU.mult).then_inc(S["mB"], 1)
                    else:
                        nc.vector.tensor_copy(dst, src).then_inc(S["mB"], 1)
                dve.wait_ge(S["mA"], 5 * b + 5)
                nc.vector.tensor_tensor(cvec[:, b, :], bank(1)[:, 0:C], wb_bc[:, :], ALU.add).then_inc(S["mB"], 1)
                mix.do(nc.vector.tensor_tensor(mp_f[:, :], bank(0)[:, 0:C], id2[:, :], ALU.add))
                nc.vector.tensor_copy(mp_h[:, b, :], mp_f[:, :]).then_inc(S["mp_hi"], 1)
                dve.wait_ge(S["mp_hi"], b + 1)
                nc.vector.tensor_tensor(mp_l[:, b, :], mp_f[:, :], mp_h[:, b, :], ALU.subtract).then_inc(S["mB"], 1)

            def mixed(r, u, w, nt):
                dve.wait_ge(S["y_done"], r + 1)
                dve.wait_ge(S["cadd"], r + 1)
                if past(r, 2):
                    dve.wait_ge(S["acc_ready"], (r - 2) * E + 1)
                src = ps_y[0:w, 0:nt * C].rearrange("p (t c) -> p t c", c=C)
                rows = res[:, bass.ds(r * NT, NT), :] if w == P else res_t[0:w, 0:nt, :]
                nc.vector.tensor_tensor(h2[u][0:w, 0:nt, :], src, rows, ALU.add).then_inc(S["y_ready"], 1)
                dve.wait_ge(S["y_ready"], r + 1)
                ln_stats(dve, h2[u][0:w, 0:nt, :], r + (G1 + 2), u, w, nt)

            def normal(r, u, w, nt):
                dve.wait_ge(S["llo"], r + G1)
                ln_normalise(dve, h2[u][0:w, 0:nt, :], r + (G1 + 2), u, w, nt)

            top = Chain(dve, "gstep", 4)
            soft = Chain(dve, "wstep", 2)

            def select(r, u, w, nt):
                top.start(r)
                dve.wait_ge(S["gate_done"], r + 1)
                g3 = gs[0:w, 0:nt, :]
                nc.vector.tensor_tensor(g3, ps_gate[0:w, 0:nt * E].rearrange("p (t e) -> p t e", e=E),
                                        bg_bc[0:w, None, :].broadcast_to([w, nt, E]), ALU.add).then_inc(S["gate_ready"], 1)
                dve.wait_ge(S["gate_ready"], r + 1)
                other = g3[:, :, None, :].broadcast_to([w, nt, E, E])
                own = g3[:, :, :, None].broadcast_to([w, nt, E, E])
                c4 = gcmp[0:w, 0:nt, :].rearrange("p t (e j) -> p t e j", j=E)
                top.do(nc.vector.tensor_tensor(c4, other, own, ALU.subtract))
                top.do(nc.vector.tensor_tensor(gcmp[0:w, 0:nt, :], gcmp[0:w, 0:nt, :],
                                               low_m[0:w, None, :].broadcast_to([w, nt, E * E]), ALU.is_gt))
                top.do(nc.vector.reduce_sum(gcnt[0:w, 0:nt * E], gcmp[0:w, 0:nt, :].rearrange("p t (e j) -> p (t e) j", j=E), AX))
                top.do(nc.vector.reduce_max(gmx[0:w, 0:nt], g3, AX))
                nc.vector.tensor_tensor(gex[0:w, 0:nt, :], g3, gmx[0:w, 0:nt, None].broadcast_to([w, nt, E]),
                                        ALU.subtract).then_inc(S["selected"], 1)

            def weigh(r, u, w, nt):
                soft.start(r)
                dve.wait_ge(S["gexp"], r + 1)
                c3 = gcnt[0:w, 0:nt * E].rearrange("p (t e) -> p t e", e=E)
                nc.vector.scalar_tensor_tensor(gex[0:w, 0:nt, :], c3, 2.0, gex[0:w, 0:nt, :], ALU.is_lt,
                                               ALU.mult).then_inc(S["gsel"], 1)
                dve.wait_ge(S["gsel"], r + 1)
                soft.do(nc.vector.reduce_sum(gsum[0:w, 0:nt], gex[0:w, 0:nt, :], AX))
                soft.do(nc.vector.reciprocal(grec[0:w, 0:nt], gsum[0:w, 0:nt]))
                if past(r, 2):
                    dve.wait_ge(S["yc_ready"], (r - 1) * E)
                nc.vector.tensor_tensor(comb[u][0:w, 0:nt, :], gex[0:w, 0:nt, :],
                                        grec[0:w, 0:nt, None].broadcast_to([w, nt, E]), ALU.mult).then_inc(S["comb_ready"], 1)

            def chunk(c, r, u, w, nt):
                e, m, n = c // NM, c % NM, w * nt
                if e < E:
                    dve.wait_ge(S["h_hi"], r * CH + (c + 1))
                    nc.vector.scalar_tensor_tensor(hl[e % 2][:, m, 0:n], z_src(e, m, n), 0.0, hh[e % 2][:, m, 0:n],
                                                   ALU.max, ALU.subtract).then_inc(S["h_lo"], 1)
            expert_blocks(dve, [(MIXED, mixed), (NORMAL, normal), (SELECT, select), (WEIGH, weigh)], chunk)

        @block.tensor
        def _(pe):
            pe.wait_ge(S["split"], 1)
            pe.wait_ge(S["zeros"], 16)
            nc.tensor.matmul(bank(7)[:, 0:C], bias_v[:, :], w2_f, start=True, stop=True).then_inc(S["vb_done"], 1)

            def qk(g, u):
                pe.wait_ge(S["xs_lo"], g * 2 + 2)
                if past(g, 1):
                    pe.wait_ge(S["q_lo"], g)
                nc.tensor.matmul(ps_k, wk_h, xs[u][:, :], start=True, stop=False)
                nc.tensor.matmul(ps_k, wk_l, xs[u][:, :], start=False, stop=True)
                nc.tensor.matmul(ps_q, wq_h, xs[u][:, :], start=True, stop=False)
                nc.tensor.matmul(ps_q, wq_l, xs[u][:, :], start=False, stop=True).then_inc(S["qk_done"], 1)

            def v(g, u):
                pe.wait_ge(S["xrep_ready"], g + 1)
                if past(g, 1):
                    pe.wait_ge(S["v_lo"], g)
                for n in range(NP):
                    toks = xrep[:, n, :, :].rearrange("p a b -> p (a b)")
                    nc.tensor.matmul(ps_v[:, n * C:n * C + C], toks, wv_h, start=True, stop=False)
                    ins = nc.tensor.matmul(ps_v[:, n * C:n * C + C], toks, wv_l, start=False, stop=True)
                ins.then_inc(S["v_done"], 1)

            def s(g, u):
                pe.wait_ge(S["qx_dve"], g + 1)
                pe.wait_ge(S["qx_act"], g + 1)
                pe.wait_ge(S["k_lo"], g + 1)
                if past(g, 2):
                    pe.wait_ge(S["sc_ready"], g - 1)
                for w in range(NW):
                    q = qx[u % 2][:, w, :, :].rearrange("p h q -> p (h q)")
                    cols = slice(w * WIN, (w + 1) * WIN)
                    nc.tensor.matmul(ps_s[u % 2][:, cols], q, k_h[:, cols], start=True, stop=False)
                    ins = nc.tensor.matmul(ps_s[u % 2][:, cols], q, k_l[:, cols], start=False, stop=True)
                ins.then_inc(S["s_done"], 1)

            def av(g, u):
                pe.wait_ge(S["px_ready"], g + 1)
                pe.wait_ge(S["v_lo"], g + 1)
                if past(g, 2):
                    pe.wait_ge(S["o_lo"], g * 2 - 2)
                for n in range(NP):
                    dst = ps_o[u % 2][:, n * 2 * WIN:(n + 1) * 2 * WIN]
                    k = 0
                    for a in range(2):
                        for part in range(2):
                            ins = nc.tensor.matmul(dst, vx[u % 2][:, n, a, :],
                                                   px[u % 2][:, part, n, a, :, :].rearrange("p w q -> p (w q)"),
                                                   start=k == 0, stop=k == 3)
                            k += 1
                ins.then_inc(S["o_done"], 1)
            attn_steps([(qk, 2), (s, 3), (v, 5), (av, 6)], pe.Fori)

            pe.wait_ge(S["o_lo"], 2 * AB)
            pe.wait_ge(S["o_hi"], 2 * AB)
            for b in range(B):
                nc.tensor.matmul(ps_g[b], x1t_t[:, B * TW:B * TW + P], wpk_h[:, 0:P + 1], start=True, stop=False,
                                 skip_group_check=True)

            def project(r, u, w, nt):
                if past(r, 2):
                    pe.wait_ge(S["h_ready"], r - 1)
                n = P if w == P else TAIL
                for t in range(nt):
                    first = r * T + r // NB * TAIL + t * P if w == P else t * TOK + NB * T
                    cols = bass.ds(first, n)
                    dst = ps_h[u][0:n, t * C:(t + 1) * C]
                    nc.tensor.matmul(dst, o_h[:, cols], w2_h, start=True, stop=False)
                    nc.tensor.matmul(dst, o_h[:, cols], w2_l, start=False, stop=False)
                    ins = nc.tensor.matmul(dst, o_l[:, cols], w2_h, start=False, stop=True)
                ins.then_inc(S["h_done"], 1)

            def turn_gram(r, u, w, nt, b):
                pe.wait_ge(S["llo"], r + 1)
                if past(r, 2):
                    pe.wait_ge(S["t_copied"], r - 1)
                for t in range(nt):
                    ins = nc.tensor.transpose(ps_t1(u)[:, t * P:t * P + w], xt[u][0:w, t, 0:P], id_h[0:w, 0:w])
                ins.then_inc(S["t_done"], 1)
                for t in range(nt):
                    ins = nc.tensor.matmul(ps_g[t if b is None else b], xt[u][0:w, t, 0:P], xt[u][0:w, t, 0:P + 1],
                                           start=False, stop=b is None, skip_group_check=True)
                ins.then_inc(S["g_done"], 1)

            for u in range(2):
                project(u, u, P, NT)
            for b in range(B):
                if b == 0:
                    for u in range(2):
                        project(u + 2, u, P, NT)
                        turn_gram(u, u, P, NT, b)
                with pe.Fori(int(b == 0), NB // 2 - (b == B - 1)) as i:
                    for u in range(2):
                        r = i * 2 + (b * NB + u)
                        project(r + 2, u, P, NT)
                        turn_gram(r, u, P, NT, b)
            project(G1, 0, TW, B)
            turn_gram(G1 - 2, 0, P, NT, B - 1)
            turn_gram(G1 - 1, 1, P, NT, B - 1)
            turn_gram(G1, 0, TW, B, None)

            for b in range(B):
                mB = MB * b
                pe.wait_ge(S["mB"], mB + 1)
                nc.tensor.matmul(bank(0)[0:1, 0:C], gcol[:, C:C + 1], id2[:, :], start=True, stop=True).then_inc(S["mA"], 1)
                pe.wait_ge(S["mB"], mB + 2)
                nc.tensor.matmul(bank(1)[0:C + 1, 0:C], gcol[:, :], gw_sb[:, :], start=True, stop=False)
                nc.tensor.matmul(bank(1)[0:C + 1, 0:C], grow[0:1, :], gb_sb[0:1, :], start=False, stop=True).then_inc(S["mA"], 1)
                pe.wait_ge(S["mB"], mB + 3)
                nc.tensor.matmul(bank(0)[0:C, 0:C], t1[:, :], th_sb[:, :], start=True, stop=True).then_inc(S["mA"], 1)
                pe.wait_ge(S["mB"], mB + 4)
                nc.tensor.matmul(bank(1)[0:C, 0:C], ft[:, :], ww_sb[:, :], start=True, stop=True).then_inc(S["mA"], 1)
                pe.wait_ge(S["mB"], mB + 5)
                nc.tensor.matmul(bank(0)[:, 0:C], ph_sb[:, :], fw[:, :], start=True, stop=True)
                nc.tensor.matmul(bank(1)[:, 0:C], phb_sb[:, :], fw[:, :], start=True, stop=True).then_inc(S["mA"], 1)
            pe.wait_ge(S["mB"], MB * B)
            pe.wait_ge(S["t_copied"], G1 + 1)
            pe.wait_ge(S["fw_prep"], 11)

            def mix(r, u, w, nt):
                if past(r, 1):
                    pe.wait_ge(S["gate_ready"], r)
                for t in range(nt):
                    if w == P:
                        toks = x1t[:, bass.ds(r, 1), t * P:(t + 1) * P].rearrange("p a b -> p (a b)")
                        m_h, m_l = (m[:, bass.ds(r // NB, 1), :].rearrange("p a c -> p (a c)") for m in (mp_h, mp_l))
                    else:
                        toks = x1t_t[:, t * TW:(t + 1) * TW]
                        m_h, m_l = mp_h[:, t, :], mp_l[:, t, :]
                    dst = ps_y[0:w, t * C:(t + 1) * C]
                    nc.tensor.matmul(dst, toks, m_h, start=True, stop=False)
                    ins = nc.tensor.matmul(dst, toks, m_l, start=False, stop=True)
                ins.then_inc(S["y_done"], 1)

            def turn(r, u, w, nt):
                pe.wait_ge(S["llo"], r + (G1 + 2))
                if past(r, 1):
                    pe.wait_ge(S["xb_ready"], r)
                for t in range(nt):
                    ins = nc.tensor.transpose(ps_t2[:, t * P:t * P + w], xt[u][0:w, t, 0:P], id_h[0:w, 0:w])
                ins.then_inc(S["t_done"], 1)

            def gate(r, u, w, nt):
                pe.wait_ge(S["xa_ready"], r + 1)
                pe.wait_ge(S["y_ready"], r + 1)
                for t in range(nt):
                    toks = xa[u][:, t * w:t * w + w]
                    dst = ps_gate[0:w, t * E:(t + 1) * E]
                    nc.tensor.matmul(dst, toks, wg_h, start=True, stop=False)
                    ins = nc.tensor.matmul(dst, toks, wg_l, start=False, stop=True)
                ins.then_inc(S["gate_done"], 1)

            def hidden(c, r, u, n):
                e, m = c // NM, c % NM
                if past(r, 1) or e >= 2:
                    pe.wait_ge(S["h_lo"], r * CH + (c + 1 - 2 * NM))
                cols = slice(c * P, (c + 1) * P)
                nc.tensor.matmul(z_src(e, m, n), w1_h[:, cols], xa[u][:, 0:n], start=True, stop=False)
                nc.tensor.matmul(z_src(e, m, n), w1_l[:, cols], xb[u][:, 0:n], start=False, stop=True).then_inc(S["z_done"], 1)

            def output(f, m, r, u, w, nt):
                k = r * E + f
                if m == 0:
                    if past(r, 1) or f >= 2:
                        pe.wait_ge(S["ye_ready"], k - 1)
                    nc.tensor.matmul(ps_ye[f % 2][:, 0:nt * C], one_rows[:, :],
                                     fb2_sb[:, None, f * C:(f + 1) * C].broadcast_to([P, nt, C]), start=True,
                                     stop=False, skip_group_check=True)
                pe.wait_ge(S["h_lo"], k * NM + (m + 1))
                for t in range(nt):
                    dst = ps_ye[f % 2][:, t * C:(t + 1) * C]
                    hi = hh[f % 2][:, m, t * w:t * w + P]
                    lo = hl[f % 2][:, m, t * w:t * w + P]
                    nc.tensor.matmul(dst, hi, f2_h[:, f * NM + m, :], start=False, stop=False, skip_group_check=True)
                    nc.tensor.matmul(dst, hi, f2_l[:, f * NM + m, :], start=False, stop=False, skip_group_check=True)
                    ins = nc.tensor.matmul(dst, lo, f2_h[:, f * NM + m, :], start=False, stop=m == NM - 1, skip_group_check=True)
                if m == NM - 1:
                    ins.then_inc(S["e_done"], 1)

            def chunk(c, r, u, w, nt):
                if c == 0:
                    pe.wait_ge(S["xb_ready"], r + 1)
                if c < CH:
                    hidden(c, r, u, w * nt)
                ready = behind(c, r, u, w, nt)
                if ready:
                    output(*ready)
            expert_blocks(pe, [(MIX, mix), (TURN, turn), (GATE, gate)], chunk)


def _f(a):
    return np.ascontiguousarray(a)


def kernel(**inputs):
    import concourse.bacc as bacc
    from concourse.bass_utils import run_bass_kernel_spmd

    v = {n: np.asarray(a) for n, a in inputs.items()}
    order = [(hp, a, e) for a in range(2) for hp in range(NH // 2) for e in range(HE)]
    v_of = np.array([e * NH + 2 * hp + a for hp, a, e in order])
    o_of = np.array([(2 * hp + a) * HE + e for hp, a, e in order])
    w1 = v["L0_tok_w1"].reshape(C, 3, C)
    b1 = v["L0_tok_b1"].reshape(C, 3)
    at = np.array([[i, j] for i in range(WS) for j in range(WS)])
    rel = at[None, :, :] - at[:, None, :] + WS - 1
    q, k = np.arange(WIN)[:, None], np.arange(WIN)[None, :]
    row = np.where((q // WS < WS // 2) != (k // WS < WS // 2), MASKED, 0.0)
    col = np.where((q % WS < WS // 2) != (k % WS < WS // 2), MASKED, 0.0)
    masks = np.zeros((WIN, 3 * WROW, WIN), np.float32)
    masks[:, 2 * WROW:, :] += row[:, None, :]
    masks[:, WROW - 1::WROW, :] += col[:, None, :]
    part = np.arange(P)
    chan = np.arange(C)

    def rows(a, n=P):
        return _f(np.broadcast_to(a.reshape(1, -1), (n, a.size)))

    arrays = {
        "x": v["x"],
        "wq": np.tile(w1[:, 0].T, (2, 2)), "wk": np.tile(w1[:, 1].T, (2, 2)), "wv": np.tile(w1[v_of, 2].T, (2, 1)),
        "bq": np.tile(b1[:, 0:1], (2, 1)), "bk": np.tile(b1[:, 1:2], (2, 1)),
        "bv": np.broadcast_to(np.concatenate([b1[v_of, 2:3], np.zeros((C, 1), np.float32)]), (P, P)),
        "w2": np.tile(v["L0_tok_w2"].T[o_of], (2, 1)), "b2": rows(v["L0_tok_b2"]),
        "pos": np.tile(v["L0_tok_pos_emb"][rel[..., 0], rel[..., 1]], (NH, 1)),
        "wmask": np.tile(masks.reshape(WIN, -1), (NH, 1)),
        "pairmask": (part[:, None] // WIN % 2 == np.arange(2)[None, :]).astype(np.float32),
        "headmask": (part[:, None] % NH == np.arange(NH)[None, :]).astype(np.float32),
        "ident": np.eye(P, dtype=np.float16), "ident2": np.tile(np.eye(C, dtype=np.float32), (2, 1)),
        "cls": np.broadcast_to(v["cls_tok"], (1, B, C)),
        "gw": np.tile(v["L0_attn_g_w"].T, (2, 1)), "gb": v["L0_attn_g_b"].reshape(1, C),
        "thw": np.concatenate([v["L0_attn_theta_w"].T, v["L0_attn_theta_b"].reshape(1, C)]),
        "phw": np.tile(v["L0_attn_phi_w"], (1, 2)), "phb": np.broadcast_to(v["L0_attn_phi_b"][:, None], (C, P)),
        "ww": v["L0_attn_W_w"].T, "wb": rows(v["L0_attn_W_b"]),
        "wg": np.tile(v["L0_ffn_Wg"].T, (2, 1)), "bg": rows(v["L0_ffn_bg"]),
        "f1": np.tile(v["L0_ffn_W1"].transpose(2, 0, 1).reshape(C, E * HID), (2, 1)),
        "fb1": v["L0_ffn_b1"].reshape(1, E * HID),
        "f2": v["L0_ffn_W2"].reshape(E, C, NM, P).transpose(3, 0, 2, 1).reshape(P, E * NM * C),
        "fb2": v["L0_ffn_b2"].reshape(1, E * C),
        "lower": rows(np.where(chan % E < chan // E, -TINY, 0.0).astype(np.float32)),
    }
    nc = bacc.Bacc("TRN2", target_bir_lowering=False, num_devices=1)
    arrays = {f"in_{n}": _f(a) for n, a in arrays.items()}
    args = {n[3:]: nc.dram_tensor(n, a.shape, mybir.dt.from_np(a.dtype), kind="ExternalInput").ap()
            for n, a in arrays.items()}
    out = nc.dram_tensor("out_dram", (B * SEQ, C), F32, kind="ExternalOutput").ap()
    swin_linattn_moe(nc, out=out, **args)
    r = run_bass_kernel_spmd(nc, [arrays], core_ids=[0])
    return r.results[0]["out_dram"].reshape(B, SEQ, C)
```

```python
from contextlib import ExitStack

import numpy as np

import concourse.bass as bass
from concourse import mybir

P = 128
F32 = mybir.dt.float32
F16 = mybir.dt.float16
ALU = mybir.AluOpType
ACT = mybir.ActivationFunctionType
AX = mybir.AxisListType.X

B, C, HT, WD = 4, 64, 56, 56
WS, NH, HE = 4, 8, 8
WIN = WS * WS
WROW = WD // WS
TOK = HT * WD
SEQ = TOK + 1
NW = 2 * WROW
NP = NW // 2
AT = NW * WIN
AB = B * (HT // WS) // 2
ABB = AB // B
T = 512
NT = T // P
NB = TOK // T
TAIL = TOK - NB * T
TW = TAIL + 1
E, HID = 8, 256
NM = HID // P
G1 = B * NB
CH = E * NM
LAG = 3
EPS = 1e-5
SCALE = 1.0 / float(np.sqrt(np.float32(C / NH)))
MASKED = -1e30
TINY = float(np.finfo(np.float32).tiny)


def swin_linattn_moe(nc, x, first, tables, late, ident, cls, f1, fb1, f2, fb2, out):
    ctx = ExitStack()
    with ctx:
        def sb(name, shape, dt=F32):
            return ctx.enter_context(nc.sbuf_tensor(name, shape, dt))

        def sem(name):
            return ctx.enter_context(nc.semaphore(name))

        def places(buf, widths):
            at = np.cumsum([0] + widths)
            return [buf[:, int(lo):int(hi)] for lo, hi in zip(at[:-1], at[1:])]
        wst = sb("first_consts", [P, first.shape[1]])
        _, _, _, w2_f, _, bias_q, bias_k, head_m, pair_m, bias_v, b2_bc = \
            places(wst, [P, P, C, C, E, 1, 1, NH, 2, P, C])
        wpk_h = sb("weights_h", [P, 3 * P + E], F16)
        wpk_l = sb("weights_l", [P, 3 * P + E], F16)
        wq_h, wk_h, wv_h, w2_h = wpk_h[:, 0:P], wpk_h[:, P:2 * P], wpk_h[:, 2 * P:2 * P + C], wpk_h[:, 2 * P + C:3 * P]
        wq_l, wk_l, wv_l, w2_l = wpk_l[:, 0:P], wpk_l[:, P:2 * P], wpk_l[:, 2 * P:2 * P + C], wpk_l[:, 2 * P + C:3 * P]
        wg_h, wg_l = wpk_h[:, 3 * P:3 * P + E], wpk_l[:, 3 * P:3 * P + E]
        score_tables = sb("score_tables", [P, 3 * WROW + 1, WIN])
        score_bias, pos_sb = score_tables[:, 0:3 * WROW, :], score_tables[:, 3 * WROW, :]
        id_h = sb("id_h", [P, P], F16)
        late_sb = sb("late_consts", [P, late.shape[1]])
        id2, gw_sb, wb_bc, bg_bc, low_m, th_sb, ph_sb, phb_sb, ww_sb, gb_sb = \
            places(late_sb, [C, C, C, E, E * E, C, P, P, C, C])
        th_sb, ph_sb, phb_sb, ww_sb, gb_sb = th_sb[0:C + 1], ph_sb[0:C], phb_sb[0:C], ww_sb[0:C], gb_sb[0:1]
        half_neg = sb("half_neg", [P, NT])
        w1_h = sb("w1_h", [P, E * HID], F16)
        w1_l = sb("w1_l", [P, E * HID], F16)
        f2_h = sb("f2_h", [P, E * NM, C], F16)
        f2_l = sb("f2_l", [P, E * NM, C], F16)
        fb2_sb = sb("fb2_sb", [P, E * C], F16)
        one_rows = sb("one_rows", [P, P], F16)
        img = sb("img", [P, 2 * HT, WD])
        xs = [sb(f"xs{i}", [P, AT], F16) for i in range(4)]
        xrep = sb("xrep", [P, NP, 4, 2 * WIN], F16)
        k_h, k_l = sb("k_h", [P, AT], F16), sb("k_l", [P, AT], F16)
        q_s = sb("q_s", [P, AT], F16)
        spread_buf = sb("spread_buf", [P, 4, NW * P], F16)
        qx = [spread_buf[:, i, :].rearrange("p (w h q) -> p w h q", h=NH, q=WIN) for i in range(2)]
        sc = [sb(f"sc{i}", [P, AT]) for i in range(2)]
        smax, ssum, srec = ([sb(f"{n}{i}", [P, NW]) for i in range(2)] for n in ("smax", "ssum", "srec"))
        prt = sb("prt", [P, AT])
        pt = sb("pt", [P, 2, AT], F16)
        pt_h, pt_l = pt[:, 0, :], pt[:, 1, :]
        px = [sb(f"px{i}", [P, 2, NP, 2, 2, WIN], F16) for i in range(2)]
        vx = [spread_buf[:, 2 + i, :].rearrange("p (n a c) -> p n a c", a=2, c=P) for i in range(2)]
        o_h = sb("o_h", [P, B * TOK], F16)
        o_l = sb("o_l", [P, B * TOK], F16)
        res = sb("res", [P, B * NB * NT, C])
        res_t = sb("res_t", [P, B, C])
        x1t = spread_buf[:, :, :].rearrange("p i n -> p (i n)")[:, 0:B * NB * T].rearrange("p (r n) -> p r n", n=T)
        x1t_t = sb("x1t_t", [P, B * TW + P], F16)
        xt = [sb(f"xt{i}", [P, NT, P + 2], F16) for i in range(2)]
        ln_s = [smax[i][:, 0:NT * 6].rearrange("p (t n) -> p t n", n=6) for i in range(2)]
        pad = sb("pad", [P, 1])
        ln_m = [sb(f"ln_m{i}", [P, NT, 2]) for i in range(2)]
        ln_v = [sb(f"ln_v{i}", [P, NT]) for i in range(2)]
        ln_r = [sb(f"ln_r{i}", [P, NT]) for i in range(2)]
        ln_n = [sb(f"ln_n{i}", [P, NT, C]) for i in range(2)]
        gcol = sb("gcol", [P, B, C + 1])
        grow = sb("grow", [1, B, C + 1])

        def by_batch(buf, rows):
            return buf[0:rows, 0:B * C].rearrange("p (b c) -> p b c", c=C)
        gright, t1, ft = by_batch(sc[0], P), by_batch(sc[1], C + 1), by_batch(prt, C)
        fw, mp_f = by_batch(sc[0], C), by_batch(sc[1], P)
        mp_h, mp_l = sb("mp_h", [P, B, C], F16), sb("mp_l", [P, B, C], F16)
        cvec = sb("cvec", [P, B, C])
        h2 = [sb(f"h2{i}", [P, NT, C]) for i in range(2)]
        xa = [sb(f"xa{i}", [P, T], F16) for i in range(2)]
        xb = [sb(f"xb{i}", [P, T], F16) for i in range(2)]
        gs = sb("gs", [P, NT, E])
        gcmp = sb("gcmp", [P, NT, E * E])
        gcnt, gmx, gex = sb("gcnt", [P, NT * E]), sb("gmx", [P, NT]), sb("gex", [P, NT, E])
        gsum, grec = sb("gsum", [P, NT]), sb("grec", [P, NT])
        comb = [sb(f"comb{i}", [P, NT, E]) for i in range(2)]
        hh = [sb(f"hh{i}", [P, NM, T], F16) for i in range(2)]
        hl = [sb(f"hl{i}", [P, NM, T], F16) for i in range(2)]
        k_f = [t[:, :, :].rearrange("p a b -> p (a b)").bitcast(F32)[:, 0:AT] for t in hh]
        ye = [sb(f"ye{i}", [P, NT, C]) for i in range(2)]
        yc = sb("yc", [P, NT, C])
        acc = [sb(f"acc{i}", [P, NT, C]) for i in range(2)]
        flat = img[:, :, :].rearrange("p a b -> p (a b)")
        w1_f = flat[:, 0:E * HID]
        f2_f = flat[:, E * HID:E * HID + E * NM * C]
        fb1_f = flat[C:P, HT * WD:HT * WD + E * HID]
        fb2_f = flat[:, HT * WD + E * HID:HT * WD + E * HID + E * C]

        ps = ctx.enter_context(nc.psum_tensor("ps", [P, 8 * 512], F32))

        def bank(i, n=1):
            return ps[:, 512 * i:512 * (i + n)]

        ps_q, ps_k, ps_v = bank(0)[:, 0:AT], bank(1)[:, 0:AT], bank(2, 2)
        ps_s = [bank(4)[:, 0:AT], bank(5)[:, 0:AT]]
        ps_o = [bank(6)[:, 0:AT], bank(7)[:, 0:AT]]
        ps_h = [bank(0), bank(1)]
        ps_g = [bank(4 + b)[:, 0:P + 1] for b in range(B)]
        ps_ye = [bank(4), bank(5)]
        ps_t2 = bank(6).bitcast(F16)[:, 0:NT * P]
        ps_y, ps_gate = bank(7)[:, 0:NT * C], bank(6)[:, NT * C:NT * C + NT * E]
        ACT_HEADS = 5

        def ps_t1(u):
            return bank(2 + u).bitcast(F16)[:, 0:NT * P]

        def z_src(e, m, n):
            return bank(2 * (e % 2) + m)[:, 0:n]

        def y_src(e, w, nt):
            return ps_ye[e % 2][0:w, 0:nt * C].rearrange("p (t c) -> p t c", c=C)

        def v_src(hp):
            return ps_v[32 * hp:32 * hp + 32, 0:NP * C].rearrange("p (n a h e) -> p n a h e", a=2, e=HE, h=NH // 2)[:, :, :, hp, :]

        def v_diag(u, hp, lo):
            base = vx[u][32 * hp:32 * hp + 32]
            return bass.AP(base.tensor, base.offset + lo * C + hp * HE,
                           [list(base.ap[0]), [2 * P, NP], [P + C // 2, 2], [1, HE]])

        def o_src(u, ip):
            return ps_o[u][:, ip * AT // 2:(ip + 1) * AT // 2].rearrange("p (j a b) -> p j a b", a=WS, b=WS)

        def o_dst(buf, g, ip):
            return buf[:, bass.ds(g * AT + ip * AT // 2, AT // 2)].rearrange("p (a j b) -> p j a b", a=WS, b=WS)

        names = ("consts tables late vx_zero img_top img w_hi split xs_ready xs_lo xrep_ready k_hi k_lo q_hi q_lo qx_dve qx_act "
                 "qk_done v_done s_done o_done v_hi v_lo sc_ready max_ready shift_ready exp_ready sum_ready rec_ready "
                 "norm_ready pt_ready pt_hi pt_lo px_ready o_hi o_lo sbias zeros "
                 "h_done h_ready lstats lmean lveps lrstd lnorm lhi llo t_done t_copied g_done "
                 "mA mB gram_right mp_sum mp_hi y_done y_ready cadd xa_ready xb_ready gate_done gate_ready "
                 "gdiff gmax gahead gshift gcount gsel gtotal grec comb_ready cls_in kept vb_done vb_ready gexp "
                 "z_done h_hi h_lo e_done ye_ready yc_ready acc_ready stored0 stored1 fw_load fw_hi fw_lo").split()
        S = {n: sem(n) for n in names}
        block = ctx.enter_context(nc.Block())

        TOP = 4 * WS

        def load_rows(eng, b, name, pieces):
            s = WS // 2
            for half in range(2):
                d = img[C * half:C * half + C, HT * (b % 2):HT * (b % 2) + HT, :]
                for dy, sy, ny in pieces:
                    for (dx, sx, nx) in ((0, s, WD - s), (WD - s, 0, s)):
                        eng.dma_start(d[:, dy:dy + ny, dx:dx + nx],
                                      x[b, :, sy:sy + ny, sx:sx + nx]).then_inc(S[name], 16)

        def load_image(eng, b):
            s = WS // 2
            if b:
                eng.wait_ge(S["img"], IMG * b)
            top = 0 if b else TOP
            load_rows(eng, b, "img", ((top, top + s, HT - s - top), (HT - s, 0, s)))

        IMG = 8 * 16

        def attn_steps(stages, loop):
            depth = max(lag for _, lag in stages)
            lead = 8

            def step(s, u, check):
                for fn, lag in stages:
                    if not check or 0 <= s - lag < AB:
                        fn(s - lag, (u - lag) % 4)
            for s in range(lead):
                step(s, s % 4, True)
            trips = (AB - lead) // 4
            with loop(0, trips) as i:
                for u in range(4):
                    step(i * 4 + (lead + u), u, False)
            for s in range(lead + 4 * trips, AB + depth):
                step(s, s % 4, True)

        def past(g, n):
            return not isinstance(g, int) or g >= n

        @block.sync
        def _(sp):
            load_rows(sp, 0, "img_top", ((0, WS // 2, TOP),))
            sp.dma_start(wst[:, :], first).then_inc(S["consts"], 16)
            sp.dma_start(score_tables[:, :, :].rearrange("p a b -> p (a b)"), tables).then_inc(S["tables"], 16)
            load_image(sp, 0)
            sp.dma_start(late_sb[:, :], late).then_inc(S["late"], 16)
            sp.dma_start(id_h[:, :], ident).then_inc(S["late"], 16)
            sp.dma_start(res_t[TAIL:TW, :, :], cls).then_inc(S["late"], 16)
            load_image(sp, 1)
            for b in range(2, B):
                sp.wait_ge(S["xs_lo"], 2 * ABB * (b - 1))
                load_image(sp, b)
            sp.wait_ge(S["xs_lo"], 2 * AB)
            sp.dma_start(w1_f, f1).then_inc(S["fw_load"], 16)
            sp.dma_start(f2_f, f2).then_inc(S["fw_load"], 16)
            sp.dma_start(fb1_f, fb1).then_inc(S["fw_load"], 16)
            sp.dma_start(fb2_f, fb2).then_inc(S["fw_load"], 16)

            def store(b, r, u, n):
                sp.wait_ge(S["acc_ready"], n)
                base = b * SEQ + 1 + r * T
                sp.dma_start(out[bass.ds(base, T), :].rearrange("(t p) c -> p t c", p=P),
                             acc[u][:, :, :]).then_inc(S[f"stored{u}"], 16)
            for b in range(B):
                with sp.Fori(0, NB // 2) as i:
                    for u in range(2):
                        r = i * 2 + u
                        store(b, r, u, E * (r + b * NB + 1))
            sp.wait_ge(S["acc_ready"], E * (B * NB + 1))
            by_entry = out.rearrange("(b s) c -> s b c", b=B)
            sp.dma_start(by_entry[1 + NB * T:SEQ], acc[0][0:TAIL, :, :]).then_inc(S["stored0"], 16)
            sp.dma_start(by_entry[0:1], acc[0][TAIL:TW, :, :]).then_inc(S["stored0"], 16)
            sp.wait_ge(S["stored0"], 16 * (G1 // 2 + 2))
            sp.wait_ge(S["stored1"], 16 * (G1 // 2))

        def ln_stats(dve, src, u, w, nt):
            for t in range(nt):
                ins = nc.vector.bn_stats(ln_s[u][0:w, t, :], src[:, t, :])
            ins.then_inc(S["lstats"], 1)

        def ln_moments(dve, m, u, w, nt):
            dve.wait_ge(S["lstats"], m)
            nc.vector.memset(pad[:, :], 0.0)
            for t in range(nt):
                ins = nc.vector.bn_aggr(ln_m[u][0:w, t, :], ln_s[u][0:w, t, :])
            ins.then_inc(S["lmean"], 1)

        def ln_epsilon(dve, m, u, w, nt):
            dve.wait_ge(S["lmean"], m)
            nc.vector.tensor_scalar(ln_v[u][0:w, 0:nt], ln_m[u][0:w, 0:nt, 1], EPS, None, ALU.add).then_inc(S["lveps"], 1)

        def ln_rstd(pool, m, u, w, nt):
            pool.wait_ge(S["lveps"], m)
            nc.gpsimd.tensor_tensor(ln_r[u][0:w, 0:nt], ln_v[u][0:w, 0:nt], half_neg[0:w, 0:nt],
                                    ALU.pow).then_inc(S["lrstd"], 1)

        def ln_normalise(dve, src, m, u, w, nt):
            dve.wait_ge(S["lrstd"], m)
            for t in range(nt):
                ins = nc.vector.tensor_scalar(ln_n[u][0:w, t, :], src[:, t, :], ln_m[u][0:w, t, 0:1],
                                              ln_r[u][0:w, t:t + 1], ALU.subtract, ALU.mult)
            ins.then_inc(S["lnorm"], 1)

        def ln_high(act, m, u, w, nt):
            act.wait_ge(S["lnorm"], m)
            nc.scalar.activation(xt[u][0:w, 0:nt, 0:C], ln_n[u][0:w, 0:nt, :], ACT.Copy).then_inc(S["lhi"], 1)

        def ln_low(pool, m, u, w, nt):
            pool.wait_ge(S["lhi"], m)
            nc.gpsimd.tensor_tensor(xt[u][0:w, 0:nt, C:P], ln_n[u][0:w, 0:nt, :], xt[u][0:w, 0:nt, 0:C],
                                    ALU.subtract).then_inc(S["llo"], 1)

        def blocks_of(engine, stages):
            shape = lambda r: (TW, B) if isinstance(r, int) and r == G1 else (P, NT)

            def step(s, u):
                for fn, lag in stages:
                    r = s - lag
                    if not isinstance(r, int) or 0 <= r <= G1:
                        fn(r, (u - lag) % 2, *shape(r))
            for s in range(4):
                step(s, s % 2)
            with engine.Fori(2, G1 // 2) as i:
                for u in range(2):
                    step(i * 2 + u, u)
            for s in range(G1, G1 + 5):
                step(s, s % 2)

        CONST, MIX, MIXED, STATS, MOMENTS, EPSILON, RSTD, NORMAL, HIGH, LOW, TURN, COLUMNS, GATE = \
            -12, -11, -10, -9, -8, -7, -6, 3, 5, 5, 8, 9, 11
        GSCORES, COMPARE, AHEAD, COUNT, GEXP, SELECT, TOTAL, WEIGH = 13, 13, 14, 15, 17, 17, 18, 18
        MB = 7

        def mix_out(i, rows):
            return bank(i)[0:rows, 0:B * C].rearrange("p (b c) -> p b c", c=C)

        def expert_blocks(engine, prep, body):
            full, tail = (P, NT), (TW, B)

            def prepare(piece, r, u):
                if not isinstance(r, int) or r <= G1:
                    piece(r, u, *(tail if isinstance(r, int) and r == G1 else full))

            def one(r, u, shape):
                for c in range(CH):
                    body(c, r, u, *shape)
                    for at, piece in prep:
                        if at % CH == c:
                            n = 1 - at // CH
                            prepare(piece, r + n, (u + n) % 2)
            for at, piece in prep:
                if at < CH:
                    prepare(piece, 0, 0)
            for at, piece in prep:
                if at < 0:
                    prepare(piece, 1, 1)
            for u in range(2):
                one(u, u, full)
            with engine.Fori(1, G1 // 2 - 1) as i:
                for u in range(2):
                    one(i * 2 + u, u, full)
            one(G1 - 2, 0, full)
            one(G1 - 1, 1, full)
            one(G1, 0, tail)
            for c in range(CH, CH + LAG):
                body(c, G1, 0, *tail)

        def behind(c, r, u, w, nt):
            c -= LAG
            if c >= 0:
                return c // NM, c % NM, r, u, w, nt
            return (c // NM + E, c % NM, r - 1, 1 - u, P, NT) if past(r, 1) else None

        @block.gpsimd
        def _(pool):
            fills = [(half_neg[:, :], -0.5),
                     (one_rows[:, :], 0.0), (x1t_t[:, B * TW:B * TW + P], 0.0)]
            fills += [(t[:, :, P:P + 2], 1.0) for t in xt] + [(t[C:P, :], 0.0) for t in xb]
            fills += [(t[r:r + 1, :], 1.0) for t in xb for r in (64, 96)] + [(one_rows[r:r + 1, :], 1.0) for r in (0, 32)]
            for n, (dst, value) in enumerate(fills):
                nc.gpsimd.memset(dst, value).then_inc(S["zeros"], 1)
                pool.wait_ge(S["zeros"], n + 1)

            def take_tokens(g, u):
                if isinstance(g, int) and g < 2:
                    pool.wait_ge(S["img_top"], 4 * 16)
                else:
                    pool.wait_ge(S["img"], IMG * (g // ABB + 1))
                if past(g, 4):
                    pool.wait_ge(S["xrep_ready"], g - 3)
                    pool.wait_ge(S["qk_done"], g - 3)
                def rows(p0, ip):
                    return img[p0:P, bass.ds(g % (2 * ABB) * (2 * WS) + ip * WS, WS), :]\
                        .rearrange("c a (j b) -> c j a b", b=WS)

                def dst(p0, ip):
                    return xs[u][p0:P, ip * AT // 2:(ip + 1) * AT // 2]\
                        .rearrange("c (j a b) -> c j a b", a=WS, b=WS)
                for ip in range(2):
                    nc.gpsimd.tensor_copy(dst(0, ip), rows(0, ip)).then_inc(S["xs_ready"], 1)
                pool.wait_ge(S["xs_ready"], g * 2 + 2)
                for ip in range(2):
                    nc.gpsimd.tensor_tensor(dst(C, ip), rows(C, ip), dst(C, ip), ALU.subtract).then_inc(S["xs_lo"], 1)
                pool.wait_ge(S["xs_lo"], g * 2 + 2)

            def shift(g, u):
                pool.wait_ge(S["max_ready"], g + 1)
                s3 = sc[u % 2][:, :].rearrange("p (w k) -> p w k", k=WIN)
                nc.gpsimd.tensor_tensor(s3, s3, smax[u % 2][:, :, None].broadcast_to([P, NW, WIN]),
                                        ALU.subtract).then_inc(S["shift_ready"], 1)

            def normalise(g, u):
                pool.wait_ge(S["rec_ready"], g + 1)
                s3 = sc[u % 2][:, :].rearrange("p (w k) -> p w k", k=WIN)
                nc.gpsimd.tensor_tensor(s3, s3, srec[u % 2][:, :, None].broadcast_to([P, NW, WIN]),
                                        ALU.mult).then_inc(S["norm_ready"], 1)

            def k_low(g, u):
                pool.wait_ge(S["k_hi"], g + 1)
                if past(g, 1):
                    pool.wait_ge(S["s_done"], g)
                nc.gpsimd.tensor_tensor(k_l[:, :], k_f[u % 2], k_h[:, :], ALU.subtract).then_inc(S["k_lo"], 1)

            def low_part(g, u):
                pool.wait_ge(S["pt_hi"], g + 1)
                if past(g, 1):
                    pool.wait_ge(S["px_ready"], g)
                nc.gpsimd.tensor_tensor(pt_l, prt[:, :], pt_h, ALU.subtract).then_inc(S["pt_lo"], 1)

            attn_steps([(low_part, 5), (normalise, 4), (shift, 3), (k_low, 2), (take_tokens, 0)], pool.Fori)

            blocks_of(pool, [(lambda r, u, w, nt: ln_rstd(pool, r + 1, u, w, nt), 1),
                             (lambda r, u, w, nt: ln_low(pool, r + 1, u, w, nt), 2)])

            pool.wait_ge(S["fw_hi"], 4)
            nc.gpsimd.tensor_tensor(w1_l[0:C, :], w1_f[0:C, :], w1_h[0:C, :], ALU.subtract).then_inc(S["fw_lo"], 1)
            nc.gpsimd.tensor_tensor(f2_l[:, :, :].rearrange("p a c -> p (a c)"), f2_f,
                                    f2_h[:, :, :].rearrange("p a c -> p (a c)"), ALU.subtract).then_inc(S["fw_lo"], 1)
            pool.wait_ge(S["kept"], G1 + 1)
            pool.wait_ge(S["fw_lo"], 4)
            pool.wait_ge(S["mB"], MB)

            def constant(r, u, w, nt):
                if w == P:
                    rows = res[:, bass.ds(r * NT, NT), :]
                    row = cvec[:, bass.ds(r // NB, 1), :].broadcast_to([P, NT, C])
                    nc.gpsimd.tensor_tensor(rows, rows, row, ALU.add).then_inc(S["cadd"], 1)
                else:
                    nc.gpsimd.tensor_tensor(res_t[0:w, :, :], res_t[0:w, :, :], cvec[0:w, :, :],
                                            ALU.add).then_inc(S["cadd"], 1)

            def rstd(r, u, w, nt):
                ln_rstd(pool, r + (G1 + 2), u, w, nt)

            def low(r, u, w, nt):
                ln_low(pool, r + (G1 + 2), u, w, nt)

            def combine(r, u, w, nt, e):
                k = r * E + e
                pool.wait_ge(S["ye_ready"], k + 1)
                if e == 0:
                    pool.wait_ge(S["comb_ready"], r + 1)
                if past(k, 1):
                    pool.wait_ge(S["acc_ready"], k)
                nc.gpsimd.tensor_tensor(yc[0:w, 0:nt, :], ye[e % 2][0:w, 0:nt, :],
                                        comb[u][0:w, 0:nt, e:e + 1].broadcast_to([w, nt, C]), ALU.mult).then_inc(S["yc_ready"], 1)
                pool.wait_ge(S["yc_ready"], k + 1)
                if e == 0 and past(r, 2):
                    pool.wait_ge(S[f"stored{u}"], r // 2 * 16)
                first = h2[u][0:w, 0:nt, :] if e == 0 else acc[u][0:w, 0:nt, :]
                nc.gpsimd.tensor_tensor(acc[u][0:w, 0:nt, :], first, yc[0:w, 0:nt, :], ALU.add).then_inc(S["acc_ready"], 1)


            def chunk(c, *block):
                done = behind(c, *block)
                if done and done[1] == NM - 1:
                    combine(*done[2:], done[0])
            expert_blocks(pool, [(CONST, constant), (RSTD, rstd), (LOW, low)], chunk)

        @block.scalar
        def _(act):
            act.wait_ge(S["consts"], 16)
            act.wait_ge(S["vx_zero"], 2)
            act.wait_ge(S["split"], 1)

            def q_high(g, u):
                act.wait_ge(S["qk_done"], g + 1)
                if past(g, 1):
                    act.wait_ge(S["qx_dve"], g)
                    act.wait_ge(S["qx_act"], g)
                nc.scalar.activation(q_s[:, :], ps_q, ACT.Identity, bias=bias_q[:, :]).then_inc(S["q_hi"], 1)

            def k_high(g, u):
                if past(g, 1):
                    act.wait_ge(S["s_done"], g)
                nc.scalar.activation(k_h[:, :], ps_k, ACT.Identity, bias=bias_k[:, :])
                if past(g, 2):
                    act.wait_ge(S["k_lo"], g - 1)
                nc.scalar.activation(k_f[u % 2], ps_k, ACT.Identity, bias=bias_k[:, :]).then_inc(S["k_hi"], 1)

            def spread(g, u):
                act.wait_ge(S["q_lo"], g + 1)
                if past(g, 2):
                    act.wait_ge(S["s_done"], g - 1)
                q3 = q_s[:, :].rearrange("p (w q) -> p w q", q=WIN)
                for h in range(ACT_HEADS):
                    ins = nc.scalar.activation(qx[u % 2][:, :, h, :], q3, ACT.Copy, scale=head_m[:, h:h + 1])
                ins.then_inc(S["qx_act"], 1)

            def v_high(g, u):
                act.wait_ge(S["v_done"], g + 1)
                if past(g, 2):
                    act.wait_ge(S["o_done"], g - 1)
                for hp in range(4):
                    nc.scalar.activation(v_diag(u % 2, hp, 0), v_src(hp), ACT.Copy).then_inc(S["v_hi"], 1)

            def exp(g, u):
                act.wait_ge(S["shift_ready"], g + 1)
                nc.scalar.activation(sc[u % 2][:, :], sc[u % 2][:, :], ACT.Exp).then_inc(S["exp_ready"], 1)

            def p_high(g, u):
                act.wait_ge(S["pt_ready"], g + 1)
                if past(g, 1):
                    act.wait_ge(S["px_ready"], g)
                nc.scalar.activation(pt_h, prt[:, :], ACT.Copy).then_inc(S["pt_hi"], 1)

            def o_high(g, u):
                act.wait_ge(S["o_done"], g + 1)
                for ip in range(2):
                    nc.scalar.activation(o_dst(o_h, g, ip), o_src(u % 2, ip), ACT.Copy).then_inc(S["o_hi"], 1)
            attn_steps([(p_high, 5), (q_high, 2), (k_high, 2), (v_high, 5), (spread, 2), (o_high, 6), (exp, 3)], act.Fori)

            act.wait_ge(S["fw_load"], 4 * 16)
            for dst, src in ((w1_h[:, :], w1_f), (w1_l[C:P, :], fb1_f), (f2_h[:, :, :].rearrange("p a c -> p (a c)"), f2_f),
                             (fb2_sb[:, :], fb2_f)):
                nc.scalar.activation(dst, src, ACT.Copy).then_inc(S["fw_hi"], 1)

            def keep(r, u, w, nt):
                act.wait_ge(S["h_ready"], r + 1)
                if w == P:
                    ins = nc.scalar.activation(res[:, bass.ds(r * NT, NT), :], h2[u][:, :, :], ACT.Copy)
                else:
                    ins = nc.scalar.activation(res_t[0:TAIL, :, :], h2[u][0:TAIL, :, :], ACT.Copy)
                ins.then_inc(S["kept"], 1)

            def high1(r, u, w, nt):
                if past(r, 2):
                    act.wait_ge(S["g_done"], r - 1)
                ln_high(act, r + 1, u, w, nt)

            def turned1(r, u, w, nt):
                act.wait_ge(S["t_done"], r + 1)
                src = ps_t1(u)
                if w == P:
                    ins = nc.scalar.activation(x1t[:, bass.ds(r, 1), :].rearrange("p a b -> p (a b)"), src, ACT.Copy)
                else:
                    ins = nc.scalar.activation(x1t_t[:, 0:B * TW].rearrange("p (t n) -> p t n", n=TW),
                                               src.rearrange("p (t n) -> p t n", n=P)[:, :, 0:TW], ACT.Copy)
                ins.then_inc(S["t_copied"], 1)
            blocks_of(act, [(turned1, 3), (high1, 2), (keep, 0)])

            def high(r, u, w, nt):
                if past(r, 2):
                    act.wait_ge(S["t_done"], r + G1)
                ln_high(act, r + (G1 + 2), u, w, nt)

            def columns(r, u, w, nt):
                act.wait_ge(S["t_done"], r + (G1 + 2))
                if past(r, 2):
                    act.wait_ge(S["z_done"], (r - 1) * (E * NM))
                    act.wait_ge(S["gate_done"], r - 1)
                src = ps_t2.rearrange("p (t n) -> p t n", n=P)[:, 0:nt, 0:w]
                n = w * nt
                nc.scalar.activation(xa[u][:, 0:n].rearrange("p (t n) -> p t n", n=w), src, ACT.Copy).then_inc(S["xa_ready"], 1)
                nc.scalar.activation(xb[u][0:C, 0:n].rearrange("p (t n) -> p t n", n=w), src[0:C], ACT.Copy).then_inc(S["xb_ready"], 1)

            def gate_exp(r, u, w, nt):
                act.wait_ge(S["gshift"], r + 1)
                nc.scalar.activation(gex[0:w, 0:nt, :], gex[0:w, 0:nt, :], ACT.Exp).then_inc(S["gexp"], 1)

            def chunk(c, r, u, w, nt):
                e, m, n = c // NM, c % NM, w * nt
                if e < E:
                    act.wait_ge(S["z_done"], r * CH + (c + 1))
                    nc.scalar.activation(hh[e % 2][:, m, 0:n], z_src(e, m, n), ACT.Relu).then_inc(S["h_hi"], 1)
                done = behind(c, r, u, w, nt)
                if done and done[1] == NM - 1:
                    f, _, q, _, w, nt = done
                    k = q * E + f
                    act.wait_ge(S["e_done"], k + 1)
                    if past(q, 1) or f >= 2:
                        act.wait_ge(S["yc_ready"], k - 1)
                    nc.scalar.activation(ye[f % 2][0:w, 0:nt, :], y_src(f, w, nt), ACT.Copy).then_inc(S["ye_ready"], 1)
            expert_blocks(act, [(HIGH, high), (COLUMNS, columns), (GEXP, gate_exp)], chunk)

        @block.vector
        def _(dve):
            for u in range(2):
                nc.vector.memset(vx[u][:, :, :, :], 0.0).then_inc(S["vx_zero"], 1)
            dve.wait_ge(S["consts"], 16)
            nf = 3 * P + E
            nc.vector.tensor_copy(wpk_h[:, 0:nf], wst[:, 0:nf]).then_inc(S["w_hi"], 1)
            dve.wait_ge(S["w_hi"], 1)
            nc.vector.tensor_tensor(wpk_l[:, 0:nf], wst[:, 0:nf], wpk_h[:, 0:nf], ALU.subtract).then_inc(S["split"], 1)
            nc.vector.memset(grow[:, :, C:C + 1], float(SEQ)).then_inc(S["sbias"], 1)
            dve.wait_ge(S["tables"], 16)
            nc.vector.tensor_tensor(score_bias, score_bias, pos_sb[:, None, :].broadcast_to([P, 3 * WROW, WIN]),
                                    ALU.add).then_inc(S["sbias"], 1)
            dve.wait_ge(S["sbias"], 2)
            dve.wait_ge(S["vx_zero"], 2)
            dve.wait_ge(S["vb_done"], 1)
            nc.vector.tensor_tensor(b2_bc[:, :], bank(7)[:, 0:C], b2_bc[:, :], ALU.add).then_inc(S["vb_ready"], 1)

            def scores(g, u):
                dve.wait_ge(S["s_done"], g + 1)
                if past(g, 2):
                    dve.wait_ge(S["pt_ready"], g - 1)
                last = g % ABB // (ABB - 1) * WROW
                nc.vector.scalar_tensor_tensor(
                    sc[u % 2][:, :].rearrange("p (w k) -> p w k", k=WIN), ps_s[u % 2].rearrange("p (w k) -> p w k", k=WIN),
                    SCALE, score_bias[:, bass.ds(last, NW), :], ALU.mult, ALU.add).then_inc(S["sc_ready"], 1)

            def maxima(g, u):
                dve.wait_ge(S["sc_ready"], g + 1)
                nc.vector.reduce_max(smax[u % 2][:, :], sc[u % 2][:, :].rearrange("p (w k) -> p w k", k=WIN), AX)\
                    .then_inc(S["max_ready"], 1)

            def replicate(g, u):
                dve.wait_ge(S["xs_lo"], g * 2 + 2)
                if past(g, 1):
                    dve.wait_ge(S["v_done"], g)
                nc.vector.tensor_copy(xrep[:, :, :, :], xs[u][:, :].rearrange("p (a b) -> p a b", b=2 * WIN)
                                      [:, :, None, :].broadcast_to([P, NP, 4, 2 * WIN])).then_inc(S["xrep_ready"], 1)

            def v_low(g, u):
                for hp in range(4):
                    dve.wait_ge(S["v_hi"], g * 4 + (hp + 1))
                    ins = nc.vector.tensor_tensor(v_diag(u % 2, hp, 1), v_src(hp), v_diag(u % 2, hp, 0), ALU.subtract)
                ins.then_inc(S["v_lo"], 1)

            def sums(g, u):
                dve.wait_ge(S["exp_ready"], g + 1)
                nc.vector.reduce_sum(ssum[u % 2][:, :], sc[u % 2][:, :].rearrange("p (w k) -> p w k", k=WIN), AX)\
                    .then_inc(S["sum_ready"], 1)

            def reciprocals(g, u):
                dve.wait_ge(S["sum_ready"], g + 1)
                nc.vector.reciprocal(srec[u % 2][:, :], ssum[u % 2][:, :]).then_inc(S["rec_ready"], 1)

            def q_low(g, u):
                dve.wait_ge(S["q_hi"], g + 1)
                nc.vector.scalar_tensor_tensor(q_s[C:P, :], ps_q[C:P], bias_q[C:P, :], q_s[C:P, :], ALU.add,
                                               ALU.subtract).then_inc(S["q_lo"], 1)

            def spread(g, u):
                dve.wait_ge(S["q_lo"], g + 1)
                if past(g, 2):
                    dve.wait_ge(S["s_done"], g - 1)
                q3 = q_s[:, :].rearrange("p (w q) -> p w q", q=WIN)
                for h in range(ACT_HEADS, NH):
                    ins = nc.vector.tensor_scalar(qx[u % 2][:, :, h, :], q3, head_m[:, h:h + 1], None, ALU.mult)
                ins.then_inc(S["qx_dve"], 1)

            def turn(g, u):
                dve.wait_ge(S["norm_ready"], g + 1)
                if past(g, 1):
                    dve.wait_ge(S["pt_lo"], g)
                nc.vector.transpose(prt[:, :], sc[u % 2][:, :]).then_inc(S["pt_ready"], 1)

            def o_low(g, u):
                dve.wait_ge(S["o_hi"], g * 2 + 2)
                for ip in range(2):
                    nc.vector.tensor_tensor(o_dst(o_l, g, ip), o_src(u % 2, ip), o_dst(o_h, g, ip),
                                            ALU.subtract).then_inc(S["o_lo"], 1)

            def pairs(g, u):
                dve.wait_ge(S["pt_lo"], g + 1)
                dve.wait_ge(S["pt_hi"], g + 1)
                if past(g, 2):
                    dve.wait_ge(S["o_done"], g - 1)
                for w in range(2):
                    ins = nc.vector.tensor_scalar(px[u % 2][:, :, :, :, w, :].rearrange("p l n a q -> p (l n a) q"),
                                                  pt[:, :, :].rearrange("p l (n q) -> p (l n) q", q=WIN),
                                                  pair_m[:, w:w + 1], None, ALU.mult)
                ins.then_inc(S["px_ready"], 1)
            attn_steps([(sums, 4), (scores, 3), (reciprocals, 4), (q_low, 2), (maxima, 3), (pairs, 5),
                        (replicate, 4), (spread, 2), (turn, 4), (v_low, 5), (o_low, 6)], dve.Fori)

            dve.wait_ge(S["vb_ready"], 1)
            dve.wait_ge(S["late"], 3 * 16)

            def ln1(r, u, w, nt):
                dve.wait_ge(S["h_done"], r + 1)
                if past(r, 2):
                    dve.wait_ge(S["kept"], r - 1)
                    dve.wait_ge(S["lnorm"], r - 1)
                n = min(w, P if w == P else TAIL)
                src = ps_h[u][0:n, 0:nt * C].rearrange("p (t c) -> p t c", c=C)
                rows = h2[u][0:w, 0:nt, :]
                if w != P:
                    nc.vector.tensor_copy(rows[n:w], res_t[n:w, :, :]).then_inc(S["cls_in"], 1)
                    dve.wait_ge(S["cls_in"], 1)
                nc.vector.tensor_tensor(rows[0:n], src, b2_bc[0:n, None, :].broadcast_to([n, nt, C]),
                                        ALU.add).then_inc(S["h_ready"], 1)

            def stats1(r, u, w, nt):
                dve.wait_ge(S["h_ready"], r + 1)
                ln_stats(dve, h2[u][0:w, 0:nt, :], u, w, nt)

            def moments1(r, u, w, nt):
                ln_moments(dve, r + 1, u, w, nt)

            def epsilon1(r, u, w, nt):
                ln_epsilon(dve, r + 1, u, w, nt)

            def normal1(r, u, w, nt):
                if past(r, 2):
                    dve.wait_ge(S["llo"], r - 1)
                ln_normalise(dve, h2[u][0:w, 0:nt, :], r + 1, u, w, nt)
            blocks_of(dve, [(moments1, 1), (normal1, 2), (epsilon1, 1), (ln1, 0), (stats1, 0)])

            dve.wait_ge(S["fw_hi"], 4)
            nc.vector.tensor_tensor(w1_l[96:97, :], fb1_f[32:33, :], w1_l[96:97, :], ALU.subtract).then_inc(S["fw_lo"], 1)
            nc.vector.tensor_tensor(fb2_sb[32:33, :], fb2_f[32:33, :], fb2_sb[32:33, :], ALU.subtract).then_inc(S["fw_lo"], 1)

            dve.wait_ge(S["g_done"], G1 + 1)
            grams = bank(4, B).rearrange("p (b n) -> p b n", n=512)
            nc.vector.tensor_copy(gright, grams[:, :, C:P]).then_inc(S["gram_right"], 1)
            dve.wait_ge(S["gram_right"], 1)
            nc.vector.tensor_copy(gcol[:, :, C:C + 1], grams[:, :, P:P + 1])
            nc.vector.tensor_tensor(gcol[:, :, 0:C], grams[:, :, 0:C], gright, ALU.add).then_inc(S["mB"], 1)
            for n, (dst, src) in enumerate(((grow[:, :, 0:C], mix_out(0, 1)), (t1, mix_out(1, C + 1)),
                                            (ft, mix_out(0, C)), (fw, mix_out(1, C)))):
                dve.wait_ge(S["mA"], n + 1)
                if n == 1:
                    nc.vector.tensor_scalar(dst, src, 1.0 / SEQ, None, ALU.mult).then_inc(S["mB"], 1)
                else:
                    nc.vector.tensor_copy(dst, src).then_inc(S["mB"], 1)
            dve.wait_ge(S["mA"], 5)
            nc.vector.tensor_tensor(mp_f, mix_out(0, P), id2[:, None, :].broadcast_to([P, B, C]),
                                    ALU.add).then_inc(S["mp_sum"], 1)
            dve.wait_ge(S["mp_sum"], 1)
            nc.vector.tensor_copy(mp_h[:, :, :], mp_f).then_inc(S["mp_hi"], 1)
            dve.wait_ge(S["mp_hi"], 1)
            nc.vector.tensor_tensor(mp_l[:, :, :], mp_f, mp_h[:, :, :], ALU.subtract).then_inc(S["mB"], 1)
            dve.wait_ge(S["mA"], 6)
            nc.vector.tensor_tensor(cvec[:, :, :], mix_out(1, P), wb_bc[:, None, :].broadcast_to([P, B, C]),
                                    ALU.add).then_inc(S["mB"], 1)

            def mixed(r, u, w, nt):
                dve.wait_ge(S["y_done"], r + 1)
                dve.wait_ge(S["cadd"], r + 1)
                if past(r, 2):
                    dve.wait_ge(S["acc_ready"], (r - 2) * E + 1)
                src = ps_y[0:w, 0:nt * C].rearrange("p (t c) -> p t c", c=C)
                rows = res[:, bass.ds(r * NT, NT), :] if w == P else res_t[0:w, 0:nt, :]
                nc.vector.tensor_tensor(h2[u][0:w, 0:nt, :], src, rows, ALU.add).then_inc(S["y_ready"], 1)

            def stats(r, u, w, nt):
                dve.wait_ge(S["y_ready"], r + 1)
                ln_stats(dve, h2[u][0:w, 0:nt, :], u, w, nt)

            def moments(r, u, w, nt):
                ln_moments(dve, r + (G1 + 2), u, w, nt)

            def epsilon(r, u, w, nt):
                ln_epsilon(dve, r + (G1 + 2), u, w, nt)

            def normal(r, u, w, nt):
                dve.wait_ge(S["llo"], r + G1)
                ln_normalise(dve, h2[u][0:w, 0:nt, :], r + (G1 + 2), u, w, nt)

            def gate_scores(r, u, w, nt):
                dve.wait_ge(S["gate_done"], r + 1)
                nc.vector.tensor_tensor(gs[0:w, 0:nt, :], ps_gate[0:w, 0:nt * E].rearrange("p (t e) -> p t e", e=E),
                                        bg_bc[0:w, None, :].broadcast_to([w, nt, E]), ALU.add).then_inc(S["gate_ready"], 1)

            def compare(r, u, w, nt):
                g3 = gs[0:w, 0:nt, :]
                other = g3[:, :, None, :].broadcast_to([w, nt, E, E])
                own = g3[:, :, :, None].broadcast_to([w, nt, E, E])
                dve.wait_ge(S["gate_ready"], r + 1)
                nc.vector.tensor_tensor(gcmp[0:w, 0:nt, :].rearrange("p t (e j) -> p t e j", j=E), other, own,
                                        ALU.subtract).then_inc(S["gdiff"], 1)
                nc.vector.reduce_max(gmx[0:w, 0:nt], g3, AX).then_inc(S["gmax"], 1)

            def ahead(r, u, w, nt):
                dve.wait_ge(S["gmax"], r + 1)
                nc.vector.tensor_tensor(gex[0:w, 0:nt, :], gs[0:w, 0:nt, :], gmx[0:w, 0:nt, None].broadcast_to([w, nt, E]),
                                        ALU.subtract).then_inc(S["gshift"], 1)
                dve.wait_ge(S["gdiff"], r + 1)
                nc.vector.tensor_tensor(gcmp[0:w, 0:nt, :], gcmp[0:w, 0:nt, :],
                                        low_m[0:w, None, :].broadcast_to([w, nt, E * E]), ALU.is_gt).then_inc(S["gahead"], 1)

            def count(r, u, w, nt):
                dve.wait_ge(S["gahead"], r + 1)
                nc.vector.reduce_sum(gcnt[0:w, 0:nt * E], gcmp[0:w, 0:nt, :].rearrange("p t (e j) -> p (t e) j", j=E),
                                     AX).then_inc(S["gcount"], 1)

            def select(r, u, w, nt):
                dve.wait_ge(S["gexp"], r + 1)
                dve.wait_ge(S["gcount"], r + 1)
                c3 = gcnt[0:w, 0:nt * E].rearrange("p (t e) -> p t e", e=E)
                nc.vector.scalar_tensor_tensor(gex[0:w, 0:nt, :], c3, 2.0, gex[0:w, 0:nt, :], ALU.is_lt,
                                               ALU.mult).then_inc(S["gsel"], 1)

            def total(r, u, w, nt):
                dve.wait_ge(S["gsel"], r + 1)
                nc.vector.reduce_sum(gsum[0:w, 0:nt], gex[0:w, 0:nt, :], AX).then_inc(S["gtotal"], 1)

            def weigh(r, u, w, nt):
                dve.wait_ge(S["gtotal"], r + 1)
                nc.vector.reciprocal(grec[0:w, 0:nt], gsum[0:w, 0:nt]).then_inc(S["grec"], 1)
                dve.wait_ge(S["grec"], r + 1)
                if past(r, 2):
                    dve.wait_ge(S["yc_ready"], (r - 1) * E)
                nc.vector.tensor_tensor(comb[u][0:w, 0:nt, :], gex[0:w, 0:nt, :],
                                        grec[0:w, 0:nt, None].broadcast_to([w, nt, E]), ALU.mult).then_inc(S["comb_ready"], 1)

            def chunk(c, r, u, w, nt):
                e, m, n = c // NM, c % NM, w * nt
                if e < E:
                    dve.wait_ge(S["h_hi"], r * CH + (c + 1))
                    nc.vector.scalar_tensor_tensor(hl[e % 2][:, m, 0:n], z_src(e, m, n), 0.0, hh[e % 2][:, m, 0:n],
                                                   ALU.max, ALU.subtract).then_inc(S["h_lo"], 1)
            expert_blocks(dve, [(MIXED, mixed), (STATS, stats), (MOMENTS, moments), (EPSILON, epsilon), (NORMAL, normal),
                                (GSCORES, gate_scores), (COMPARE, compare), (AHEAD, ahead), (COUNT, count), (SELECT, select),
                                (TOTAL, total), (WEIGH, weigh)], chunk)

        @block.tensor
        def _(pe):
            pe.wait_ge(S["split"], 1)
            pe.wait_ge(S["zeros"], 13)
            nc.tensor.matmul(bank(7)[:, 0:C], bias_v[:, :], w2_f, start=True, stop=True).then_inc(S["vb_done"], 1)

            def qk(g, u):
                pe.wait_ge(S["xs_lo"], g * 2 + 2)
                if past(g, 1):
                    pe.wait_ge(S["q_lo"], g)
                    pe.wait_ge(S["k_hi"], g)
                nc.tensor.matmul(ps_k, wk_h, xs[u][:, :], start=True, stop=False)
                nc.tensor.matmul(ps_k, wk_l, xs[u][:, :], start=False, stop=True)
                nc.tensor.matmul(ps_q, wq_h, xs[u][:, :], start=True, stop=False)
                nc.tensor.matmul(ps_q, wq_l, xs[u][:, :], start=False, stop=True).then_inc(S["qk_done"], 1)

            def v(g, u):
                pe.wait_ge(S["xrep_ready"], g + 1)
                if past(g, 1):
                    pe.wait_ge(S["v_lo"], g)
                for n in range(NP):
                    toks = xrep[:, n, :, :].rearrange("p a b -> p (a b)")
                    nc.tensor.matmul(ps_v[:, n * C:n * C + C], toks, wv_h, start=True, stop=False)
                    ins = nc.tensor.matmul(ps_v[:, n * C:n * C + C], toks, wv_l, start=False, stop=True)
                ins.then_inc(S["v_done"], 1)

            def s(g, u):
                pe.wait_ge(S["qx_dve"], g + 1)
                pe.wait_ge(S["qx_act"], g + 1)
                pe.wait_ge(S["k_lo"], g + 1)
                if past(g, 2):
                    pe.wait_ge(S["sc_ready"], g - 1)
                for w in range(NW):
                    q = qx[u % 2][:, w, :, :].rearrange("p h q -> p (h q)")
                    cols = slice(w * WIN, (w + 1) * WIN)
                    nc.tensor.matmul(ps_s[u % 2][:, cols], q, k_h[:, cols], start=True, stop=False)
                    ins = nc.tensor.matmul(ps_s[u % 2][:, cols], q, k_l[:, cols], start=False, stop=True)
                ins.then_inc(S["s_done"], 1)

            def av(g, u):
                pe.wait_ge(S["px_ready"], g + 1)
                pe.wait_ge(S["v_lo"], g + 1)
                if past(g, 2):
                    pe.wait_ge(S["o_lo"], g * 2 - 2)
                for n in range(NP):
                    dst = ps_o[u % 2][:, n * 2 * WIN:(n + 1) * 2 * WIN]
                    k = 0
                    for a in range(2):
                        for part in range(2):
                            ins = nc.tensor.matmul(dst, vx[u % 2][:, n, a, :],
                                                   px[u % 2][:, part, n, a, :, :].rearrange("p w q -> p (w q)"),
                                                   start=k == 0, stop=k == 3)
                            k += 1
                ins.then_inc(S["o_done"], 1)
            attn_steps([(qk, 2), (s, 3), (v, 5), (av, 6)], pe.Fori)

            pe.wait_ge(S["o_lo"], 2 * AB)
            pe.wait_ge(S["o_hi"], 2 * AB)
            pe.wait_ge(S["late"], 3 * 16)
            for b in range(B):
                nc.tensor.matmul(ps_g[b], x1t_t[:, B * TW:B * TW + P], wpk_h[:, 0:P + 1], start=True, stop=False,
                                 skip_group_check=True)

            def project(r, u, w, nt):
                if past(r, 2):
                    pe.wait_ge(S["h_ready"], r - 1)
                n = P if w == P else TAIL
                for t in range(nt):
                    first = r * T + r // NB * TAIL + t * P if w == P else t * TOK + NB * T
                    cols = bass.ds(first, n)
                    dst = ps_h[u][0:n, t * C:(t + 1) * C]
                    nc.tensor.matmul(dst, o_h[:, cols], w2_h, start=True, stop=False)
                    nc.tensor.matmul(dst, o_h[:, cols], w2_l, start=False, stop=False)
                    ins = nc.tensor.matmul(dst, o_l[:, cols], w2_h, start=False, stop=True)
                ins.then_inc(S["h_done"], 1)

            def turn_gram(r, u, w, nt, b):
                pe.wait_ge(S["llo"], r + 1)
                if past(r, 2):
                    pe.wait_ge(S["t_copied"], r - 1)
                for t in range(nt):
                    ins = nc.tensor.transpose(ps_t1(u)[:, t * P:t * P + w], xt[u][0:w, t, 0:P], id_h[0:w, 0:w])
                ins.then_inc(S["t_done"], 1)
                for t in range(nt):
                    ins = nc.tensor.matmul(ps_g[t if b is None else b], xt[u][0:w, t, 0:P], xt[u][0:w, t, 0:P + 1],
                                           start=False, stop=b is None, skip_group_check=True)
                ins.then_inc(S["g_done"], 1)

            for r in range(3):
                project(r, r % 2, P, NT)
            for b in range(B):
                if b == 0:
                    for u in range(2):
                        project(u + 3, 1 - u, P, NT)
                        turn_gram(u, u, P, NT, b)
                with pe.Fori(int(b == 0), NB // 2 - 2 * (b == B - 1)) as i:
                    for u in range(2):
                        r = i * 2 + (b * NB + u)
                        project(r + 3, 1 - u, P, NT)
                        turn_gram(r, u, P, NT, b)
            for r in range(G1 - 4, G1):
                if r + 3 <= G1:
                    project(r + 3, (r + 3) % 2, *((P, NT) if r + 3 < G1 else (TW, B)))
                turn_gram(r, r % 2, P, NT, B - 1)
            turn_gram(G1, 0, TW, B, None)

            pe.wait_ge(S["mB"], 1)
            for b in range(B):
                ins = nc.tensor.matmul(mix_out(0, 1)[:, b, :], gcol[:, b, C:C + 1], id2[:, :], start=True, stop=True)
            ins.then_inc(S["mA"], 1)
            pe.wait_ge(S["mB"], 2)
            for b in range(B):
                nc.tensor.matmul(mix_out(1, C + 1)[:, b, :], gcol[:, b, :], gw_sb[:, :], start=True, stop=False)
                ins = nc.tensor.matmul(mix_out(1, C + 1)[:, b, :], grow[0:1, b, :], gb_sb[0:1, :], start=False, stop=True)
            ins.then_inc(S["mA"], 1)
            pe.wait_ge(S["mB"], 3)
            for b in range(B):
                ins = nc.tensor.matmul(mix_out(0, C)[:, b, :], t1[:, b, :], th_sb[:, :], start=True, stop=True)
            ins.then_inc(S["mA"], 1)
            pe.wait_ge(S["mB"], 4)
            for b in range(B):
                ins = nc.tensor.matmul(mix_out(1, C)[:, b, :], ft[:, b, :], ww_sb[:, :], start=True, stop=True)
            ins.then_inc(S["mA"], 1)
            pe.wait_ge(S["mB"], 5)
            for b in range(B):
                ins = nc.tensor.matmul(mix_out(0, P)[:, b, :], ph_sb[:, :], fw[:, b, :], start=True, stop=True)
            ins.then_inc(S["mA"], 1)
            for b in range(B):
                ins = nc.tensor.matmul(mix_out(1, P)[:, b, :], phb_sb[:, :], fw[:, b, :], start=True, stop=True)
            ins.then_inc(S["mA"], 1)
            pe.wait_ge(S["mB"], MB)
            pe.wait_ge(S["t_copied"], G1 + 1)
            pe.wait_ge(S["fw_lo"], 4)

            def mix(r, u, w, nt):
                if past(r, 1):
                    pe.wait_ge(S["y_ready"], r)
                for t in range(nt):
                    if w == P:
                        toks = x1t[:, bass.ds(r, 1), t * P:(t + 1) * P].rearrange("p a b -> p (a b)")
                        m_h, m_l = (m[:, bass.ds(r // NB, 1), :].rearrange("p a c -> p (a c)") for m in (mp_h, mp_l))
                    else:
                        toks = x1t_t[:, t * TW:(t + 1) * TW]
                        m_h, m_l = mp_h[:, t, :], mp_l[:, t, :]
                    dst = ps_y[0:w, t * C:(t + 1) * C]
                    nc.tensor.matmul(dst, toks, m_h, start=True, stop=False)
                    ins = nc.tensor.matmul(dst, toks, m_l, start=False, stop=True)
                ins.then_inc(S["y_done"], 1)

            def turn(r, u, w, nt):
                pe.wait_ge(S["llo"], r + (G1 + 2))
                if past(r, 1):
                    pe.wait_ge(S["gate_ready"], r)
                for t in range(nt):
                    ins = nc.tensor.transpose(ps_t2[:, t * P:t * P + w], xt[u][0:w, t, 0:P], id_h[0:w, 0:w])
                ins.then_inc(S["t_done"], 1)

            def gate(r, u, w, nt):
                pe.wait_ge(S["xb_ready"], r + 1)
                for t in range(nt):
                    toks = xa[u][:, t * w:t * w + w]
                    dst = ps_gate[0:w, t * E:(t + 1) * E]
                    nc.tensor.matmul(dst, toks, wg_h, start=True, stop=False)
                    ins = nc.tensor.matmul(dst, toks, wg_l, start=False, stop=True)
                ins.then_inc(S["gate_done"], 1)

            def hidden(c, r, u, n):
                e, m = c // NM, c % NM
                if past(r, 1) or e >= 2:
                    pe.wait_ge(S["h_lo"], r * CH + (c + 1 - 2 * NM))
                cols = slice(c * P, (c + 1) * P)
                nc.tensor.matmul(z_src(e, m, n), w1_h[:, cols], xa[u][:, 0:n], start=True, stop=False)
                nc.tensor.matmul(z_src(e, m, n), w1_l[:, cols], xb[u][:, 0:n], start=False, stop=True).then_inc(S["z_done"], 1)

            def output(f, m, r, u, w, nt):
                k = r * E + f
                if m == 0:
                    if past(r, 1) or f >= 2:
                        pe.wait_ge(S["ye_ready"], k - 1)
                    nc.tensor.matmul(ps_ye[f % 2][:, 0:nt * C], one_rows[:, :],
                                     fb2_sb[:, None, f * C:(f + 1) * C].broadcast_to([P, nt, C]), start=True,
                                     stop=False, skip_group_check=True)
                pe.wait_ge(S["h_lo"], k * NM + (m + 1))
                for t in range(nt):
                    dst = ps_ye[f % 2][:, t * C:(t + 1) * C]
                    hi = hh[f % 2][:, m, t * w:t * w + P]
                    lo = hl[f % 2][:, m, t * w:t * w + P]
                    nc.tensor.matmul(dst, hi, f2_h[:, f * NM + m, :], start=False, stop=False, skip_group_check=True)
                    nc.tensor.matmul(dst, hi, f2_l[:, f * NM + m, :], start=False, stop=False, skip_group_check=True)
                    ins = nc.tensor.matmul(dst, lo, f2_h[:, f * NM + m, :], start=False, stop=m == NM - 1, skip_group_check=True)
                if m == NM - 1:
                    ins.then_inc(S["e_done"], 1)

            def chunk(c, r, u, w, nt):
                if c == 0:
                    pe.wait_ge(S["xb_ready"], r + 1)
                if c < CH:
                    hidden(c, r, u, w * nt)
                ready = behind(c, r, u, w, nt)
                if ready:
                    output(*ready)
            expert_blocks(pe, [(MIX, mix), (TURN, turn), (GATE, gate)], chunk)


def _f(a):
    return np.ascontiguousarray(a)


def kernel(**inputs):
    import concourse.bacc as bacc
    from concourse.bass_utils import run_bass_kernel_spmd

    v = {n: np.asarray(a) for n, a in inputs.items()}
    order = [(hp, a, e) for a in range(2) for hp in range(NH // 2) for e in range(HE)]
    v_of = np.array([e * NH + 2 * hp + a for hp, a, e in order])
    o_of = np.array([(2 * hp + a) * HE + e for hp, a, e in order])
    w1 = v["L0_tok_w1"].reshape(C, 3, C)
    b1 = v["L0_tok_b1"].reshape(C, 3)
    at = np.array([[i, j] for i in range(WS) for j in range(WS)])
    rel = at[None, :, :] - at[:, None, :] + WS - 1
    q, k = np.arange(WIN)[:, None], np.arange(WIN)[None, :]
    row = np.where((q // WS < WS // 2) != (k // WS < WS // 2), MASKED, 0.0)
    col = np.where((q % WS < WS // 2) != (k % WS < WS // 2), MASKED, 0.0)
    masks = np.zeros((WIN, 3 * WROW, WIN), np.float32)
    masks[:, 2 * WROW:, :] += row[:, None, :]
    masks[:, WROW - 1::WROW, :] += col[:, None, :]
    part = np.arange(P)
    chan = np.arange(C)

    def rows(a, n=P):
        return _f(np.broadcast_to(a.reshape(1, -1), (n, a.size)))

    def filled(a):
        return np.concatenate([a, np.zeros((P - a.shape[0], a.shape[1]), a.dtype)])

    def padded(a, n, at):
        out = np.zeros((n, a.size), a.dtype)
        for row in at:
            out[row] = a.reshape(-1)
        return out

    arrays = {
        "x": v["x"],
        "first": np.concatenate([
            np.tile(w1[:, 0].T, (2, 2)), np.tile(w1[:, 1].T, (2, 2)), np.tile(w1[v_of, 2].T, (2, 1)),
            np.tile(v["L0_tok_w2"].T[o_of], (2, 1)), np.tile(v["L0_ffn_Wg"].T, (2, 1)),
            np.tile(b1[:, 0:1], (2, 1)), np.tile(b1[:, 1:2], (2, 1)),
            (part[:, None] % NH == np.arange(NH)[None, :]).astype(np.float32),
            (part[:, None] // WIN % 2 == np.arange(2)[None, :]).astype(np.float32),
            np.broadcast_to(np.concatenate([b1[v_of, 2:3], np.zeros((C, 1), np.float32)]), (P, P)),
            rows(v["L0_tok_b2"])], 1),
        "tables": np.concatenate([np.tile(masks.reshape(WIN, -1), (NH, 1)),
                                  np.tile(v["L0_tok_pos_emb"][rel[..., 0], rel[..., 1]], (NH, 1))], 1),
        "late": np.concatenate([
            np.tile(np.eye(C, dtype=np.float32), (2, 1)), np.tile(v["L0_attn_g_w"].T, (2, 1)), rows(v["L0_attn_W_b"]),
            rows(v["L0_ffn_bg"]), rows(np.where(chan % E < chan // E, -TINY, 0.0).astype(np.float32)),
            filled(np.concatenate([v["L0_attn_theta_w"].T, v["L0_attn_theta_b"].reshape(1, C)])),
            filled(np.tile(v["L0_attn_phi_w"], (1, 2))), filled(np.broadcast_to(v["L0_attn_phi_b"][:, None], (C, P))),
            filled(v["L0_attn_W_w"].T), filled(v["L0_attn_g_b"].reshape(1, C))], 1),
        "ident": np.eye(P, dtype=np.float16),
        "cls": np.broadcast_to(v["cls_tok"], (1, B, C)),
        "f1": np.tile(v["L0_ffn_W1"].transpose(2, 0, 1).reshape(C, E * HID), (2, 1)),
        "fb1": padded(v["L0_ffn_b1"], C, (0, 32)),
        "f2": v["L0_ffn_W2"].reshape(E, C, NM, P).transpose(3, 0, 2, 1).reshape(P, E * NM * C),
        "fb2": padded(v["L0_ffn_b2"], P, (0, 32)),
    }
    nc = bacc.Bacc("TRN2", target_bir_lowering=False, num_devices=1)
    arrays = {f"in_{n}": _f(a) for n, a in arrays.items()}
    args = {n[3:]: nc.dram_tensor(n, a.shape, mybir.dt.from_np(a.dtype), kind="ExternalInput").ap()
            for n, a in arrays.items()}
    out = nc.dram_tensor("out_dram", (B * SEQ, C), F32, kind="ExternalOutput").ap()
    swin_linattn_moe(nc, out=out, **args)
    r = run_bass_kernel_spmd(nc, [arrays], core_ids=[0])
    return r.results[0]["out_dram"].reshape(B, SEQ, C)
```
